# Optimizing a Trainium2 kernel written in Bass

```python
import numpy as np
import jax
import jax.numpy as jnp

def _softmax(x, axis=-1):
    return jax.nn.softmax(x, axis=axis)

def _gelu(x):
    return jax.nn.gelu(x, approximate=True)

def _silu(x):
    return jax.nn.silu(x)

def _sigmoid(x):
    return jax.nn.sigmoid(x)

def _layernorm(x, axis=-1, eps=1e-05):
    m = jnp.mean(x, axis=axis, keepdims=True)
    v = jnp.var(x, axis=axis, keepdims=True)
    return (x - m) / jnp.sqrt(v + eps)

def _scatter_add(tgt, idx, src, axis=0):
    return tgt.at[idx].add(src)

def _segment_sum(src, seg, n):
    return jax.ops.segment_sum(src, seg, n)
kernel_name = 'mk_gnn_preln_d1_gnn_r32_5732be'

def setup_inputs(seed: int=0):
    np.random.seed(seed)
    _w = jnp.asarray

    def _rec_inputs():
        import jax
        import jax.numpy as jnp
        _gk = jax.random.key(seed)
        x = -8.776e-05 + 1 * jax.random.normal(jax.random.fold_in(_gk, 1), (3125, 256), jnp.float32)
        _s = jax.random.randint(jax.random.fold_in(_gk, 2), (25000,), 0, 3125, jnp.int32)
        _d = jax.random.randint(jax.random.fold_in(_gk, 3), (25000,), 0, 3125, jnp.int32)
        _loop = jnp.arange(3125, dtype=jnp.int32)
        src = jnp.concatenate([_s, _d, _loop])
        dst = jnp.concatenate([_d, _s, _loop])
        _o = jnp.argsort(dst, stable=True)
        src = src[_o]
        dst = dst[_o]
        edge_attr_10 = jax.random.uniform(jax.random.fold_in(_gk, 13), (53125, 10), jnp.float32, 0.0, 1)
        edge_attr_4 = 0.000924777 + 0.999162 * jax.random.normal(jax.random.fold_in(_gk, 14), (53125, 4), jnp.float32)
        node_vec1 = jax.random.uniform(jax.random.fold_in(_gk, 15), (3125, 1), jnp.float32, 0.0, 1)
        return (x, src, dst, edge_attr_10, edge_attr_4, node_vec1)
    x, src, dst, edge_attr_10, edge_attr_4, node_vec1 = _rec_inputs()

    def _L0_gnn_setup():
        import jax, jax.numpy as jnp
        import numpy as np
        import math
        N_NODES = 625
        N_EDGES = 10000
        MUL = 64
        N_BASIS = 10
        N_HID = 100
        W_NUMEL = 4 * MUL

        def _split(x):
            s = x[..., :MUL]
            v = x[..., MUL:].reshape(x.shape[:-1] + (MUL, 3))
            return (s, v)

        def _fctp(s, v, W0, W1, attr, fan_in):
            inv = 1.0 / math.sqrt(fan_in)
            o0 = jnp.einsum('nu,uk->nk', s, W0) * attr * inv
            o1 = jnp.einsum('num,uk->nkm', v, W1) * attr[..., None] * inv
            return (o0, o1)
        key = jax.random.key(seed)
        ks = jax.random.split(key, 16)
        node_input = jax.random.normal(ks[0], (N_NODES, 4 * MUL), dtype=jnp.float32)
        node_attr = jnp.ones((N_NODES, 1), dtype=jnp.float32)
        node_deg = jax.random.randint(ks[1], (N_NODES, 1), 1, 33).astype(jnp.float32)
        edge_src = jax.random.randint(ks[2], (N_EDGES,), 0, N_NODES)
        edge_dst = jax.random.randint(ks[3], (N_EDGES,), 0, N_NODES)
        edge_attr = jax.random.normal(ks[4], (N_EDGES, 4), dtype=jnp.float32)
        edge_length_embedded = jax.random.uniform(ks[5], (N_EDGES, N_BASIS), dtype=jnp.float32)
        W_li0 = jax.random.normal(ks[6], (MUL, MUL), dtype=jnp.float32)
        W_li1 = jax.random.normal(ks[7], (MUL, MUL), dtype=jnp.float32)
        W_lm0 = jax.random.normal(ks[8], (MUL, MUL), dtype=jnp.float32)
        W_lm1 = jax.random.normal(ks[9], (MUL, MUL), dtype=jnp.float32)
        W_mlp1 = jax.random.normal(ks[10], (N_BASIS, N_HID), dtype=jnp.float32)
        W_mlp2 = jax.random.normal(ks[11], (N_HID, W_NUMEL), dtype=jnp.float32)
        W_lo0 = jax.random.normal(ks[12], (2 * MUL, MUL), dtype=jnp.float32)
        W_lo1 = jax.random.normal(ks[13], (2 * MUL, MUL), dtype=jnp.float32)
        return dict(node_input=node_input, node_attr=node_attr, node_deg=node_deg, edge_attr=edge_attr, edge_length_embedded=edge_length_embedded, W_li0=W_li0, W_li1=W_li1, W_lm0=W_lm0, W_lm1=W_lm1, W_mlp1=W_mlp1, W_mlp2=W_mlp2, W_lo0=W_lo0, W_lo1=W_lo1, edge_src=edge_src, edge_dst=edge_dst)
    _L0_gnn_all = _L0_gnn_setup()
    _L0_gnn_in = {k: v for k, v in _L0_gnn_all.items() if k in ('W_li0', 'W_li1', 'W_lm0', 'W_lm1', 'W_mlp1', 'W_mlp2', 'W_lo0', 'W_lo1')}
    del _L0_gnn_all
    return {'x': x, 'src': src, 'dst': dst, 'edge_attr_10': edge_attr_10, 'edge_attr_4': edge_attr_4, 'node_vec1': node_vec1, 'L0_gnn_W_li0': _L0_gnn_in['W_li0'], 'L0_gnn_W_li1': _L0_gnn_in['W_li1'], 'L0_gnn_W_lm0': _L0_gnn_in['W_lm0'], 'L0_gnn_W_lm1': _L0_gnn_in['W_lm1'], 'L0_gnn_W_mlp1': _L0_gnn_in['W_mlp1'], 'L0_gnn_W_mlp2': _L0_gnn_in['W_mlp2'], 'L0_gnn_W_lo0': _L0_gnn_in['W_lo0'], 'L0_gnn_W_lo1': _L0_gnn_in['W_lo1']}

def reference(x, src, dst, edge_attr_10, edge_attr_4, node_vec1, L0_gnn_W_li0, L0_gnn_W_li1, L0_gnn_W_lm0, L0_gnn_W_lm1, L0_gnn_W_mlp1, L0_gnn_W_mlp2, L0_gnn_W_lo0, L0_gnn_W_lo1):
    import jax
    import jax.numpy as jnp

    def _L0_gnn_ref(node_input, node_attr, node_deg, edge_attr, edge_length_embedded, W_li0, W_li1, W_lm0, W_lm1, W_mlp1, W_mlp2, W_lo0, W_lo1, edge_src, edge_dst):
        import jax, jax.numpy as jnp
        import numpy as np
        import math
        N_NODES = 625
        N_EDGES = 10000
        MUL = 64
        N_BASIS = 10
        N_HID = 100
        W_NUMEL = 4 * MUL

        def _split(x):
            s = x[..., :MUL]
            v = x[..., MUL:].reshape(x.shape[:-1] + (MUL, 3))
            return (s, v)

        def _fctp(s, v, W0, W1, attr, fan_in):
            inv = 1.0 / math.sqrt(fan_in)
            o0 = jnp.einsum('nu,uk->nk', s, W0) * attr * inv
            o1 = jnp.einsum('num,uk->nkm', v, W1) * attr[..., None] * inv
            return (o0, o1)
        N = node_input.shape[0]
        x0, x1 = _split(node_input)
        f0, f1 = _fctp(x0, x1, W_li0, W_li1, node_attr, MUL)
        deg_isqrt = 1.0 / jnp.sqrt(node_deg)
        f0 = f0 * deg_isqrt
        f1 = f1 * deg_isqrt[..., None]
        m0, m1 = _fctp(x0, x1, W_lm0, W_lm1, node_attr, MUL)
        h = jax.nn.silu(edge_length_embedded @ W_mlp1 / math.sqrt(N_BASIS))
        ew = h @ W_mlp2 / math.sqrt(N_HID)
        wa, wb, wc, wd = (ew[:, :MUL], ew[:, MUL:2 * MUL], ew[:, 2 * MUL:3 * MUL], ew[:, 3 * MUL:])
        g0 = f0[edge_src]
        g1 = f1[edge_src]
        y0 = edge_attr[:, 0]
        y1 = edge_attr[:, 1:4]
        m0a = wa * g0 * y0[:, None]
        m0b = wb * jnp.einsum('eum,em->eu', g1, y1) / math.sqrt(3.0)
        m1a = wc[:, :, None] * g0[:, :, None] * y1[:, None, :]
        m1b = wd[:, :, None] * g1 * y0[:, None, None]
        s_mid = jax.ops.segment_sum(jnp.concatenate([m0a, m0b], axis=1), edge_dst, num_segments=N)
        v_mid = jax.ops.segment_sum(jnp.concatenate([m1a, m1b], axis=1), edge_dst, num_segments=N)
        s_mid = s_mid * deg_isqrt
        v_mid = v_mid * deg_isqrt[..., None]
        o0, o1 = _fctp(s_mid, v_mid, W_lo0, W_lo1, node_attr, 2 * MUL)
        c_s, c_x = (math.sin(math.pi / 8), math.cos(math.pi / 8))
        out0 = c_s * m0 + c_x * o0
        out1 = c_s * m1 + c_x * o1
        return jnp.concatenate([out0, out1.reshape(N, 3 * MUL)], axis=1)
    deg = jnp.maximum(jax.ops.segment_sum(jnp.ones(dst.shape, jnp.float32), dst, num_segments=3125), 1.0)
    h = jnp.maximum(_layernorm(x, axis=-1), 0.0)
    x = x + _L0_gnn_ref(h, node_vec1, deg[:, None], edge_attr_4, edge_attr_10, L0_gnn_W_li0, L0_gnn_W_li1, L0_gnn_W_lm0, L0_gnn_W_lm1, L0_gnn_W_mlp1, L0_gnn_W_mlp2, L0_gnn_W_lo0, L0_gnn_W_lo1, src, dst)
    return x

_drawn_inputs = setup_inputs


def setup_inputs(seed=0):
    import zlib

    import numpy as np

    out = dict(_drawn_inputs(seed))
    spreads = {}
    factors = {'edge_attr_10': 6.221,
     'edge_attr_4': 2.882,
     'L0_gnn_W_li0': 3.881,
     'L0_gnn_W_li1': 4.391,
     'L0_gnn_W_mlp1': 2.767,
     'L0_gnn_W_mlp2': 2.934,
     'L0_gnn_W_lo0': 5.569,
     'L0_gnn_W_lo1': 3.324,
     'L0_gnn_W_lm0': 43.349,
     'L0_gnn_W_lm1': 24.156}
    for name, (base, spread) in spreads.items():
        noise = np.random.default_rng([zlib.crc32(name.encode()), seed]).standard_normal(out[name].shape)
        drawn = base * np.exp(spread * noise) if base else spread * noise
        out[name] = jnp.asarray(drawn.astype(out[name].dtype))
    for name, factor in factors.items():
        out[name] = (out[name] * factor).astype(out[name].dtype)
    return out
```

```python
import math
from contextlib import ExitStack

import concourse.bass as bass
from concourse import mybir

NODES, EDGES, MUL, BASIS, HID = 3125, 53125, 64, 10, 100
P = 128
WIDTH = 4 * MUL
NT = -(-NODES // P)
NODES_PAD = NT * P
BODY = 16
ET = -(-EDGES // (P * BODY)) * BODY
EDGES_PAD = ET * P
ET_FULL = EDGES // P
LAST_EDGES = EDGES - ET_FULL * P
ITERS = ET // BODY
HALF = BODY // 2
WIN = 16
LO = 64
HI = 50
GROUPS = 5
BLOCKS = 9
SLOTS = HALF
EPS = 1e-5
C_S, C_X = math.sin(math.pi / 8), math.cos(math.pi / 8)


def gnn_layer(nc, x_nodes, src_t, dst_t, el_t, edge_y, attr_t, w_li0, w_li1, w_lm0, w_lm1, w_mlp1, w_mlp2,
              w_lo0, w_lo1, out):
    f32, bf16, i32 = mybir.dt.float32, mybir.dt.bfloat16, mybir.dt.int32
    ALU, ACT, AX = mybir.AluOpType, mybir.ActivationFunctionType, mybir.AxisListType

    ctx = ExitStack()
    with ctx:
        def sb(name, shape, dt=f32):
            return ctx.enter_context(nc.sbuf_tensor(name, shape, dt))

        def sem(name):
            return ctx.enter_context(nc.semaphore(name))

        table = nc.dram_tensor("table", (NODES_PAD, WIDTH), f32, kind="Internal").ap()

        ACC = GROUPS * NODES_PAD
        arena = sb("arena", [P, (LO + HI) * ET // 2])
        onehot = arena[:, 0:(LO + HI) * ET // 2].bitcast(bf16).rearrange("p (j t) -> p j t", t=ET)
        acc = arena[:, 0:ACC].rearrange("p (g n) -> p g n", g=GROUPS)
        f_rows = arena[:, ACC:ACC + NT * WIDTH].rearrange("p (t f) -> p t f", t=NT)
        g_rows = arena[:, ACC:ACC + SLOTS * WIDTH].rearrange("p (s f) -> p s f", s=SLOTS)
        at = ACC + SLOTS * WIDTH
        XB = 2
        prods = arena[:, at:at + XB * 2 * BLOCKS * MUL].rearrange("p (s t b u) -> p s t b u", s=XB, t=2, b=BLOCKS)

        x_sb = sb("x_sb", [P, NT, WIDTH])
        hT = sb("hT", [P, NT, WIDTH])
        stats = sb("stats", [P, NT, 6])
        mean_var = sb("mean_var", [P, NT, 2])
        std = sb("std", [P, NT])
        rstd = sb("rstd", [P, NT])
        shift = sb("shift", [P, NT])
        normed = sb("normed", [P, 4, WIDTH])
        ident = sb("ident", [P, P])
        ones = sb("ones", [P, P])
        iota = sb("iota", [P, P])
        attr = sb("attr", [P, NT])
        deg = sb("deg", [P, NT])
        sdeg = sb("sdeg", [P, NT])
        isq = sb("isq", [P, NT])
        c_f = sb("c_f", [P, NT])
        c_m = sb("c_m", [P, NT])
        c_o = sb("c_o", [P, NT])
        a8 = sb("a8", [P, NT])
        src_i = sb("src_i", [P, ET], i32)
        dst_i = sb("dst_i", [P, ET], i32)
        hi_i = sb("hi_i", [P, ET], i32)
        lo_i = sb("lo_i", [P, ET], i32)
        hi_b = sb("hi_b", [P, ET], bf16)
        lo_b = sb("lo_b", [P, ET], bf16)
        dst_f = sb("dst_f", [P, ET])
        rel = sb("rel", [P, ET])
        below = sb("below", [P, ET])
        outside = sb("outside", [P, ET])
        any_out = sb("any_out", [P, 1])
        flag = sb("flag", [1, 1], i32)
        bases = sb("bases", [1, ET + 2 + BODY], i32)
        y_sb = sb("y_sb", [P, ET, 4])
        li_a = sb("li_a", [P, P])
        li_b = sb("li_b", [P, P])
        lm_a = sb("lm_a", [P, P])
        lm_b = sb("lm_b", [P, P])
        lo_w = sb("lo_w", [P, 4, P])
        twice = sb("twice", [LO, 2 * LO])
        hist = sb("hist", [LO, HI])
        w1 = sb("w1", [BASIS, HID])
        w2_raw = sb("w2_raw", [HID, WIDTH])
        w2 = sb("w2", [HID, WIDTH])
        idx = sb("idx", [P, 2, HALF], i32)
        el = sb("el", [BASIS, 2, HALF * P])
        hid = sb("hid", [HID, 2, 4 * P])
        oh = sb("oh", [P, 2, HALF, WIN])
        sel = sb("sel", [P, 2, HALF, 4, WIN])
        o_sb = sb("o_sb", [P, 4, WIDTH])
        slow_sel = sb("slow_sel", [P, 4, P])
        slow_dst = sb("slow_dst", [P, 1])

        bank = [ctx.enter_context(nc.psum_tensor(f"bank{i}", [P, 512], f32)) for i in range(8)]
        hist_ps = bank[0][0:LO, 0:HI]
        deg_ps = bank[0][:, 128:128 + HI]
        out_ps = bank[0][0:1, 64:65]
        base_ps = bank[1][:, 0:ET]
        hid_ps = bank[0:2]
        ew_ps = [b[:, :].rearrange("p (t f) -> p t f", t=2) for b in bank[2:6]]
        msg_ps = [b[:, 0:2 * GROUPS * WIN].rearrange("p (t g j) -> p t g j", t=2, g=GROUPS) for b in bank[6:8]]

        zeroed = sem("zeroed")
        consts = sem("consts")
        dst_in, src_in, y_in, attr_in, w_in = (sem(n) for n in ("dst_in", "src_in", "y_in", "attr_in", "w_in"))
        x_in = [sem(f"x_in{c}") for c in range(5)]
        v_step = sem("v_step")
        base_mm, hist_mm, out_mm = sem("base_mm"), sem("hist_mm"), sem("out_mm")
        hist_ready, deg_mm = sem("hist_ready"), sem("deg_mm")
        dstf_ready, onehots_ready, anyout_ready = sem("dstf_ready"), sem("onehots_ready"), sem("anyout_ready")
        stats_ready, std_ready, normed_ready = sem("stats_ready"), sem("std_ready"), sem("normed_ready")
        trans_done, hT_ready, f_done, f_scaled = sem("trans_done"), sem("hT_ready"), sem("f_done"), sem("f_scaled")
        m_done, res_done = sem("m_done"), sem("res_done")
        deg_ready, sdeg_ready, cf_ready = sem("deg_ready"), sem("sdeg_ready"), sem("cf_ready")
        flag_ready, w2_ready, acc_zeroed, bases_ready = (sem(n) for n in ("flag_ready", "w2_ready", "acc_zeroed", "bases_ready"))
        table_out = sem("table_out")
        acc_ready = sem("acc_ready")
        fin_mm, fin_done = sem("fin_mm"), sem("fin_done")
        o_out = [sem(f"o_out{i}") for i in range(4)]
        el_ready = [sem(f"el_ready{b}") for b in range(2)]
        gathered = [sem(f"gathered{s}") for s in range(SLOTS)]
        idx_ready, hid_mm, silu_done, ew_mm = sem("idx_ready"), sem("hid_mm"), sem("silu_done"), sem("ew_mm")
        prod_done, msg_mm, add_done, oh_done, sel_ready = (sem(n) for n in ("prod_done", "msg_mm", "add_done", "oh_done", "sel_ready"))
        g_el, g_idx, g_row, g_hid, g_silu, g_ew, g_prod, g_sel, g_msg, g_add, g_chain = (
            sem("g_" + n) for n in ("el", "idx", "row", "hid", "silu", "ew", "prod", "sel", "msg", "add", "chain"))

        block = ctx.enter_context(nc.Block())
        NW = 18

        def flagged(eng):
            eng.wait_ge(flag_ready, 1)
            return eng.value_load(flag[0:1, 0:1], min_val=0, max_val=1)

        @block.sync
        def _(sp):
            sp.dma_start(dst_i[:, :], dst_t).then_inc(dst_in, 16)
            x_v = x_nodes.rearrange("(t p) f -> p t f", p=P)
            for c in range(5):
                sp.dma_start(x_sb[:, 5 * c:5 * c + 5, :], x_v[:, 5 * c:5 * c + 5, :]).then_inc(x_in[c], 16)
            sp.dma_start(src_i[:, :], src_t).then_inc(src_in, 16)
            sp.dma_start(y_sb[:, :, :], edge_y.rearrange("p (t k) -> p t k", k=4)).then_inc(y_in, 16)
            t_v = table.rearrange("(t p) f -> p t f", p=P)
            for c in range(5):
                sp.wait_ge(f_scaled, 5 * c + 5)
                sp.dma_start(t_v[:, 5 * c:5 * c + 5, :], f_rows[:, 5 * c:5 * c + 5, :]).then_inc(table_out, 16)

            def load_el(i, b):
                sp.dma_start(el[:, b, :], el_t[:, bass.ds((i * 2 + b) * HALF * P, HALF * P)]).then_inc(el_ready[b], 16)

            fl = flagged(sp)
            with sp.If(fl == 0):
                load_el(0, 0)
                load_el(0, 1)
                with sp.Fori(1, ITERS) as i:
                    for b in range(2):
                        sp.wait_ge(hid_mm, i * 4 + (2 * b - 2))
                        load_el(i, b)
            with sp.Else():
                sp.dma_start(el[:, 0, 0:P], el_t[:, 0:P]).then_inc(g_el, 16)
                with sp.Fori(1, ET) as t:
                    sp.wait_ge(g_hid, t)
                    sp.dma_start(el[:, 0, 0:P], el_t[:, bass.ds(t * P, P)]).then_inc(g_el, 16)

            o_v = out.rearrange("(t p) f -> t p f", p=P)
            for t in range(NT):
                sp.wait_ge(fin_done, t + 1)
                sp.dma_start(o_v[t, :, :], o_sb[:, t % 4, :]).then_inc(o_out[t % 4], 16)
            for s in range(4):
                sp.wait_ge(o_out[s], 16 * len(range(s, NT, 4)))

        @block.gpsimd
        def _(pool):
            for w in (li_a, li_b, lm_a, lm_b):
                nc.gpsimd.memset(w[:, :], 0.0).then_inc(zeroed, 1)
            nc.gpsimd.memset(lo_w[:, :, :], 0.0).then_inc(zeroed, 1)
            nc.gpsimd.memset(ones[:, :], 1.0).then_inc(consts, 1)
            nc.gpsimd.iota(iota[:, :], pattern=[[1, P]], base=0, channel_multiplier=0,
                           allow_small_or_imprecise_dtypes=True).then_inc(consts, 1)
            nc.gpsimd.memset(ident[:, :], 0.0).then_inc(consts, 1)
            pool.wait_ge(consts, 3)
            nc.gpsimd.affine_select(out=ident[:, :], in_=ident[:, :], compare_op=ALU.not_equal, fill=1.0, base=0,
                                    pattern=[[-1, P]], channel_multiplier=1).then_inc(consts, 1)
            pool.wait_ge(consts, 4)
            for h in range(2):
                nc.gpsimd.tensor_copy(twice[:, h * LO:h * LO + LO], ident[0:LO, 0:LO]).then_inc(consts, 1)
            pool.wait_ge(hist_mm, 1)
            nc.gpsimd.memset(acc, 0.0).then_inc(acc_zeroed, 1)
            pool.wait_ge(src_in, 16)
            fl = flagged(pool)

            counts = [pool.alloc_register(f"count_{n}") for n in range(2)]

            def value(v, n):
                if isinstance(v, int):
                    return v
                pool.reg_mov(counts[n], v)
                return counts[n]

            def copy_idx(i, b):
                nc.gpsimd.tensor_copy(idx[:, b, :], src_i[:, bass.ds((i * 2 + b) * HALF, HALF)]).then_inc(idx_ready, 1)

            def body(i, first):
                for k in range(BODY):
                    b = k // HALF
                    if k % HALF == 0:
                        copy_idx(i, b)
                    copied = value(i * 2 + (b + 1), 0)
                    used = value(i * (BODY // 2) + ((k - SLOTS) // 2 + 1), 1)
                    pool.wait_ge(table_out, 5 * 16)
                    if k % HALF == 0:
                        pool.wait_ge(idx_ready, copied)
                    if not (first and k < SLOTS):
                        pool.wait_ge(prod_done, used)
                    nc.gpsimd.indirect_dma_start(
                        g_rows[:, k % SLOTS, :], None, table[:, :],
                        bass.IndirectOffsetOnAxis(idx[:, b, k % HALF:k % HALF + 1], 0)).then_inc(gathered[k % SLOTS], 16)

            with pool.If(fl == 0):
                body(0, True)
                with pool.Fori(1, ITERS) as i:
                    body(i, False)
            with pool.Else():
                def one_tile(t):
                    if not isinstance(t, int):
                        pool.wait_ge(g_prod, t)
                    nc.gpsimd.tensor_copy(idx[:, 0, 0:1], src_i[:, bass.ds(t, 1)]).then_inc(g_idx, 1)
                    copied = value(t + 1, 0)
                    pool.wait_ge(table_out, 5 * 16)
                    pool.wait_ge(g_idx, copied)
                    nc.gpsimd.indirect_dma_start(g_rows[:, 0, :], None, table[:, :],
                                                 bass.IndirectOffsetOnAxis(idx[:, 0, 0:1], 0)).then_inc(g_row, 16)

                one_tile(0)
                with pool.Fori(1, ET) as t:
                    one_tile(t)

        @block.tensor
        def _(pe):
            pe.wait_ge(consts, 6)
            pe.wait_ge(dstf_ready, 1)
            nc.tensor.matmul(base_ps, ones[0:1, :], dst_f[0:1, :], start=True, stop=True).then_inc(base_mm, 1)
            pe.wait_ge(onehots_ready, 1)
            for t in range(ET_FULL + 1):
                n = P if t < ET_FULL else LAST_EDGES
                last = nc.tensor.matmul(hist_ps, onehot[0:n, 0:LO, t], onehot[0:n, LO:LO + HI, t],
                                        start=(t == 0), stop=(t == ET_FULL))
            last.then_inc(hist_mm, 1)
            pe.wait_ge(hist_ready, 1)
            nc.tensor.matmul(deg_ps, twice[:, :], hist[:, :], start=True, stop=True).then_inc(deg_mm, 1)
            pe.wait_ge(w_in, NW * 16)

            def transposes(t):
                pe.wait_ge(normed_ready, t + 1)
                if t >= 2:
                    pe.wait_ge(hT_ready, t - 1)
                for h in range(2):
                    last = nc.tensor.transpose(bank[6 + t % 2][:, h * P:h * P + P],
                                               normed[:, t % 4, h * P:h * P + P], ident[:, :])
                last.then_inc(trans_done, 1)

            def project(t, banks, wa, wb, freed, done):
                if t >= 2:
                    pe.wait_ge(freed, t - 1)
                for h, w in enumerate((wa, wb)):
                    last = nc.tensor.matmul(banks[t % 2][:, h * P:h * P + P], hT[:, t, h * P:h * P + P], w[:, :],
                                            start=True, stop=True)
                last.then_inc(done, 1)

            for t in range(NT + 2):
                if t < NT:
                    transposes(t)
                if t >= 2:
                    pe.wait_ge(hT_ready, t - 1)
                    project(t - 2, bank[2:4], li_a, li_b, f_scaled, f_done)
            pe.wait_ge(anyout_ready, 1)
            nc.tensor.matmul(out_ps, any_out[:, :], ones[:, 0:1], start=True, stop=True).then_inc(out_mm, 1)
            for t in range(NT):
                project(t, bank[4:6], lm_a, lm_b, res_done, m_done)

            fl = flagged(pe)
            pe.wait_ge(w2_ready, 1)

            def hidden(i, c):
                b = c // 2
                if c % 2 == 0:
                    pe.wait_ge(el_ready[b], i * 16 + 16)
                if not (isinstance(i, int) and 4 * i + c < 2):
                    pe.wait_ge(silu_done, i * 4 + (c - 1))
                nc.tensor.matmul(hid_ps[c % 2][0:HID, :], w1[:, :], el[:, b, (c % 2) * 512:(c % 2) * 512 + 512],
                                 start=True, stop=True).then_inc(hid_mm, 1)

            def edge_weights(i, q):
                g = q // 2
                if q % 2 == 0:
                    pe.wait_ge(silu_done, i * 4 + (g + 1))
                if not (isinstance(i, int) and 8 * i + q < 4):
                    pe.wait_ge(prod_done, i * 8 + (q - 3))
                for tt in range(2):
                    e0 = (q % 2) * 2 * P + tt * P
                    last = nc.tensor.matmul(ew_ps[q % 4][:, tt, :], hid[:, g % 2, e0:e0 + P], w2[:, :],
                                            start=True, stop=True)
                last.then_inc(ew_mm, 1)

            def messages(i, q):
                pe.wait_ge(prod_done, i * 8 + (q + 1))
                if q % 4 == 0:
                    pe.wait_ge(sel_ready, i * 2 + (q // 4 + 1))
                if not (isinstance(i, int) and 8 * i + q < 2):
                    pe.wait_ge(add_done, i * 16 + 2 * (q - 1))
                for tt in range(2):
                    T = 2 * q + tt
                    pr = prods[:, q % 2, tt, :, :].rearrange("p b u -> p (b u)")
                    s = sel[:, (T // HALF) % 2, T % HALF, :, :]
                    for n, (block, m, k, g) in enumerate(MESSAGES):
                        last = nc.tensor.matmul(msg_ps[q % 2][0:m, tt, g, :], pr[:, block * MUL:block * MUL + m], s[:, k, :],
                                                start=True, stop=True)
                last.then_inc(msg_mm, 1)

            def body(i):
                for c in range(4):
                    hidden(i, c)
                    for q in (2 * c - 2, 2 * c - 1):
                        if not (isinstance(i, int) and q < 0):
                            edge_weights(*at_pair(i, q))
                        if not (isinstance(i, int) and q < 1):
                            messages(*at_pair(i, q - 1))

            with pe.If(fl == 0):
                body(0)
                with pe.Fori(1, ITERS) as i:
                    body(i)
                edge_weights(ITERS - 1, 6)
                messages(ITERS - 1, 5)
                edge_weights(ITERS - 1, 7)
                messages(ITERS - 1, 6)
                messages(ITERS - 1, 7)
            with pe.Else():
                with pe.Fori(0, ET) as t:
                    pe.wait_ge(g_el, t * 16 + 16)
                    nc.tensor.matmul(hid_ps[0][0:HID, 0:P], w1[:, :], el[:, 0, 0:P],
                                     start=True, stop=True).then_inc(g_hid, 1)
                    pe.wait_ge(g_silu, t + 1)
                    nc.tensor.matmul(ew_ps[0][:, 0, :], hid[:, 0, 0:P], w2[:, :], start=True, stop=True).then_inc(g_ew, 1)
                    pe.wait_ge(acc_zeroed, 1)
                    pe.wait_ge(g_prod, t + 1)
                    with pe.Fori(0, NT) as w:
                        pe.wait_ge(g_sel, t * NT + w + 1)
                        pr = prods[:, 0, 0, :, :].rearrange("p b u -> p (b u)")
                        for block, m, k, g in GENERAL:
                            into = bank[6][0:m, g * P:g * P + P] if g < 4 else bank[7][0:m, 0:P]
                            last = nc.tensor.matmul(into, pr[:, block * MUL:block * MUL + m], slow_sel[:, k, :],
                                                    start=True, stop=True)
                        last.then_inc(g_msg, 1)

            pe.wait_ge(acc_ready, 1)
            for t in range(NT):
                o_ps = bank[t % 4]
                if t >= 4:
                    pe.wait_ge(fin_done, t - 3)
                cols = o_ps[:, 0:WIDTH].rearrange("p (j u) -> p j u", j=4)
                for n, (g, w, j) in enumerate(((0, 0, slice(0, 2)), (3, 1, slice(2, 4)), (1, 2, slice(0, 2)),
                                               (2, 3, slice(0, 3, 2)), (4, 2, slice(0, 4, 3)))):
                    last = nc.tensor.matmul(cols[:, j, :], acc[:, g, t * P:t * P + P],
                                            lo_w[:, w, :].rearrange("p (j u) -> p j u", j=2),
                                            start=(n == 0), stop=(n == GROUPS - 1))
                last.then_inc(fin_mm, 1)

        @block.scalar
        def _(act):
            act.dma_start(attr[:, :], attr_t).then_inc(attr_in, 16)
            act.dma_start(w1[:, :], w_mlp1).then_inc(w_in, 16)
            act.dma_start(w2_raw[:, :], w_mlp2).then_inc(w_in, 16)
            act.wait_ge(zeroed, 5)
            A, B = slice(0, MUL), slice(MUL, P)
            act.dma_start(li_a[A, A], w_li0).then_inc(w_in, 16)
            act.dma_start(li_a[B, B], w_li1).then_inc(w_in, 16)
            act.dma_start(li_b[A, A], w_li1).then_inc(w_in, 16)
            act.dma_start(li_b[B, B], w_li1).then_inc(w_in, 16)
            act.dma_start(lm_a[A, A], w_lm0).then_inc(w_in, 16)
            act.dma_start(lm_a[B, B], w_lm1).then_inc(w_in, 16)
            act.dma_start(lm_b[A, A], w_lm1).then_inc(w_in, 16)
            act.dma_start(lm_b[B, B], w_lm1).then_inc(w_in, 16)
            act.dma_start(lo_w[A, 0, A], w_lo0[0:MUL, :]).then_inc(w_in, 16)
            act.dma_start(lo_w[B, 0, B], w_lo1[MUL:P, :]).then_inc(w_in, 16)
            act.dma_start(lo_w[A, 1, A], w_lo1[MUL:P, :]).then_inc(w_in, 16)
            act.dma_start(lo_w[B, 1, B], w_lo1[MUL:P, :]).then_inc(w_in, 16)
            act.dma_start(lo_w[A, 2, A], w_lo0[MUL:P, :]).then_inc(w_in, 16)
            act.dma_start(lo_w[B, 2, B], w_lo1[0:MUL, :]).then_inc(w_in, 16)
            act.dma_start(lo_w[A, 3, B], w_lo1[0:MUL, :]).then_inc(w_in, 16)
            act.dma_start(lo_w[B, 3, A], w_lo0[MUL:P, :]).then_inc(w_in, 16)

            act.wait_ge(stats_ready, 1)
            nc.scalar.activation(std[:, :], mean_var[:, :, 1], ACT.Sqrt).then_inc(std_ready, 1)
            act.wait_ge(deg_ready, 1)
            nc.scalar.activation(sdeg[:, :], deg[:, :], ACT.Sqrt).then_inc(sdeg_ready, 1)
            for t in range(NT + 2):
                if t < NT:
                    act.wait_ge(trans_done, t + 1)
                    nc.scalar.activation(hT[:, t, :], bank[6 + t % 2][:, 0:WIDTH], ACT.Relu).then_inc(hT_ready, 1)
                if t == 1:
                    act.wait_ge(cf_ready, 1)
                if t >= 2:
                    act.wait_ge(f_done, t - 1)
                    nc.scalar.activation(f_rows[:, t - 2, :], bank[2 + t % 2][:, 0:WIDTH], ACT.Copy,
                                         scale=c_f[:, t - 2:t - 1]).then_inc(f_scaled, 1)

            fl = flagged(act)

            def silu(i, c):
                act.wait_ge(hid_mm, i * 4 + (c + 1))
                if not (isinstance(i, int) and 4 * i + c < 2):
                    act.wait_ge(ew_mm, i * 8 + (2 * c - 2))
                nc.scalar.activation(hid[:, c % 2, :], hid_ps[c % 2][0:HID, :], ACT.Silu,
                                     scale=1.0 / math.sqrt(BASIS)).then_inc(silu_done, 1)

            with act.If(fl == 0):
                for c in range(4):
                    silu(0, c)
                with act.Fori(1, ITERS) as i:
                    for c in range(4):
                        silu(i, c)
            with act.Else():
                def one_tile(t):
                    act.wait_ge(g_hid, t + 1)
                    if not isinstance(t, int):
                        act.wait_ge(g_ew, t)
                    nc.scalar.activation(hid[:, 0, 0:P], hid_ps[0][0:HID, 0:P], ACT.Silu,
                                         scale=1.0 / math.sqrt(BASIS)).then_inc(g_silu, 1)

                one_tile(0)
                with act.Fori(1, ET) as t:
                    one_tile(t)

        @block.vector
        def _(dve):
            chain = [0]

            def link(ins):
                chain[0] += 1
                ins.then_inc(v_step, 1)
                dve.wait_ge(v_step, chain[0])

            dve.wait_ge(dst_in, 16)
            nc.vector.tensor_copy(dst_f[:, :], dst_i[:, :]).then_inc(dstf_ready, 1)
            nc.vector.tensor_scalar(hi_i[:, :], dst_i[:, :], 6, None, ALU.arith_shift_right)
            link(nc.vector.tensor_scalar(lo_i[:, :], dst_i[:, :], LO - 1, None, ALU.bitwise_and))
            nc.vector.tensor_copy(lo_b[:, :], lo_i[:, :])
            link(nc.vector.tensor_copy(hi_b[:, :], hi_i[:, :]))
            for j in range(LO):
                nc.vector.tensor_scalar(onehot[:, j, :], lo_b[:, :], float(j), None, ALU.is_equal)
            for j in range(HI):
                last = nc.vector.tensor_scalar(onehot[:, LO + j, :], hi_b[:, :], float(j), None, ALU.is_equal)
            last.then_inc(onehots_ready, 1)

            for t in range(NT):
                if t % 5 == 0:
                    dve.wait_ge(x_in[t // 5], 16)
                last = nc.vector.bn_stats(stats[:, t, :], x_sb[:, t, :])
            link(last)
            for t in range(NT):
                last = nc.vector.bn_aggr(mean_var[:, t, :], stats[:, t, :])
            link(last)
            nc.vector.tensor_scalar(mean_var[:, :, 1], mean_var[:, :, 1], EPS, None, ALU.add).then_inc(stats_ready, 1)
            dve.wait_ge(std_ready, 1)
            link(nc.vector.reciprocal(rstd[:, :], std[:, :]))
            link(nc.vector.scalar_tensor_tensor(shift[:, :], mean_var[:, :, 0], -1.0, rstd[:, :], ALU.mult, ALU.mult))

            def normalise(t):
                if t >= 4:
                    dve.wait_ge(trans_done, t - 3)
                nc.vector.tensor_scalar(normed[:, t % 4, :], x_sb[:, t, :], rstd[:, t:t + 1], shift[:, t:t + 1],
                                        ALU.mult, ALU.add).then_inc(normed_ready, 1)

            for t in range(4):
                normalise(t)

            link(nc.vector.memset(deg[:, :], 1.0))
            dve.wait_ge(hist_mm, 1)
            nc.vector.tensor_copy(hist[:, :], hist_ps).then_inc(hist_ready, 1)
            dve.wait_ge(deg_mm, 1)
            pairs = deg_ps.rearrange("p (t r) -> p t r", r=2)
            nc.vector.tensor_scalar(deg[0:MUL, 0:NT], pairs[0:MUL, 0:NT, 0], 1.0, None, ALU.max)
            nc.vector.tensor_scalar(deg[MUL:P, 0:NT], pairs[MUL:P, 0:NT, 1], 1.0, None, ALU.max).then_inc(deg_ready, 1)
            dve.wait_ge(attr_in, 16)
            dve.wait_ge(sdeg_ready, 1)
            nc.vector.tensor_scalar(a8[:, :], attr[:, :], 1.0 / math.sqrt(MUL), None, ALU.mult)
            link(nc.vector.reciprocal(isq[:, :], sdeg[:, :]))
            nc.vector.tensor_tensor(c_f[:, :], a8[:, :], isq[:, :], ALU.mult).then_inc(cf_ready, 1)
            nc.vector.tensor_scalar(c_m[:, :], a8[:, :], C_S, None, ALU.mult)
            dve.wait_ge(cf_ready, 1)
            link(nc.vector.tensor_scalar(c_o[:, :], c_f[:, :], C_X * math.sqrt(MUL) / math.sqrt(2 * MUL), None, ALU.mult))

            for t in range(4, 12):
                normalise(t)

            dve.wait_ge(base_mm, 1)
            link(nc.vector.tensor_tensor(rel[:, :], dst_f[:, :], base_ps, ALU.subtract))
            nc.vector.memset(outside[:, :], 0.0)
            link(nc.vector.tensor_scalar(below[:, :], rel[:, :], 0.0, None, ALU.is_lt))
            for n, cols in ((P, slice(0, ET_FULL)), (LAST_EDGES, slice(ET_FULL, ET_FULL + 1))):
                last = nc.vector.scalar_tensor_tensor(outside[0:n, cols], rel[0:n, cols], WIN - 0.5, below[0:n, cols],
                                                      ALU.is_gt, ALU.add)
            link(last)
            nc.vector.reduce_max(any_out[:, :], outside[:, :], AX.X).then_inc(anyout_ready, 1)
            link(nc.vector.memset(bases[:, :], 0))
            nc.vector.tensor_copy(bases[0:1, 2:2 + ET], dst_i[0:1, :]).then_inc(bases_ready, 1)

            dve.wait_ge(w_in, NW * 16)
            k = 1.0 / math.sqrt(HID)
            for n, (o, s) in enumerate(((0, k), (2, k), (3, k), (1, k / math.sqrt(3.0)))):
                last = nc.vector.tensor_scalar(w2[:, n * MUL:(n + 1) * MUL], w2_raw[:, o * MUL:(o + 1) * MUL], s, None, ALU.mult)
            last.then_inc(w2_ready, 1)
            for t in range(12, NT):
                normalise(t)
            dve.wait_ge(out_mm, 1)
            nc.vector.tensor_scalar(flag[:, :], out_ps, 1.0, None, ALU.min).then_inc(flag_ready, 1)
            for t in range(NT):
                dve.wait_ge(m_done, t + 1)
                nc.vector.scalar_tensor_tensor(x_sb[:, t, :], bank[4 + t % 2][:, 0:WIDTH], c_m[:, t:t + 1], x_sb[:, t, :],
                                               ALU.mult, ALU.add).then_inc(res_done, 1)

            fl = flagged(dve)
            dve.wait_ge(y_in, 16)
            dve.wait_ge(consts, 4)
            dve.wait_ge(acc_zeroed, 1)
            dve.wait_ge(bases_ready, 1)

            def select(i, b):
                T0 = (i * 2 + b) * HALF
                n = [P, HALF, WIN]
                nc.vector.tensor_tensor(oh[:, b, :, :], iota[:, 0:WIN].unsqueeze(1).broadcast_to(n),
                                        rel[:, bass.ds(T0, HALF)].unsqueeze(2).broadcast_to(n),
                                        ALU.is_equal).then_inc(oh_done, 1)
                if not (isinstance(i, int) and i == 0):
                    dve.wait_ge(msg_mm, i * 8 + 4 * (b - 1))
                dve.wait_ge(oh_done, i * 2 + (b + 1))
                n = [P, HALF, 4, WIN]
                nc.vector.tensor_tensor(sel[:, b, :, :, :], oh[:, b, :, :].unsqueeze(2).broadcast_to(n),
                                        y_sb[:, bass.ds(T0, HALF), :].unsqueeze(3).broadcast_to(n),
                                        ALU.mult).then_inc(sel_ready, 1)

            def products(i, q):
                dve.wait_ge(ew_mm, i * 8 + (q + 1))
                for s in ((2 * q) % SLOTS, (2 * q + 1) % SLOTS):
                    dve.wait_ge(gathered[s], i * 32 + 16 * (q // 4 + 1))
                if not (isinstance(i, int) and 8 * i + q < XB):
                    dve.wait_ge(msg_mm, i * 8 + (q + 1 - XB))
                multiply(prods[:, q % XB], ew_ps[q % 4], (2 * q) % SLOTS, 2).then_inc(prod_done, 1)

            def multiply(pr, ew, s0, tiles):
                g0 = g_rows[:, s0:s0 + tiles, 0:MUL]
                n = [P, tiles, 2, MUL]
                nc.vector.tensor_tensor(pr[:, 0:tiles, 0:6:5, :], ew[:, 0:tiles, 0:2 * MUL].rearrange("p t (b u) -> p t b u", b=2),
                                        g0.unsqueeze(2).broadcast_to(n), ALU.mult)
                g1 = g_rows[:, s0:s0 + tiles, MUL:].rearrange("p t (m u) -> p t m u", m=3)
                n = [P, tiles, 3, MUL]
                for w, blocks in ((2, slice(1, 4)), (3, slice(4, 9, 2))):
                    last = nc.vector.tensor_tensor(pr[:, 0:tiles, blocks, :],
                                                   ew[:, 0:tiles, w * MUL:(w + 1) * MUL].unsqueeze(2).broadcast_to(n),
                                                   g1, ALU.mult)
                return last

            def adds(i, q, base):
                dve.wait_ge(msg_mm, i * 8 + (q + 1))
                for tt in range(2):
                    T = 2 * q + tt
                    if not (isinstance(i, int) and 16 * i + T < 1):
                        dve.wait_ge(add_done, i * 16 + T)
                    win = acc[:, :, bass.ds(base[tt], WIN)]
                    nc.vector.tensor_tensor(win, win, msg_ps[q % 2][:, tt, :, :], ALU.add).then_inc(add_done, 1)

            base_regs = [dve.alloc_register(f"base_{k}") for k in range(BODY)]

            def load_bases(at, n):
                regs = base_regs[0:n]
                dve.load(regs, bases[0:1, at if isinstance(at, slice) else bass.ds(at, n)])
                return [dve.snap(r, min_val=0, max_val=NODES - 1) for r in regs]

            def body(i):
                base = load_bases(i * BODY, BODY)
                for q in range(8):
                    if q % 4 == 0:
                        select(i, q // 4)
                    products(i, q)
                    if not (isinstance(i, int) and q == 0):
                        adds(*at_pair(i, q - 1), base[2 * q:2 * q + 2])

            with dve.If(fl == 0):
                body(0)
                with dve.Fori(1, ITERS) as i:
                    body(i)
                adds(ITERS - 1, 7, load_bases(ITERS * BODY, 2))
                dve.wait_ge(add_done, ET)
                nc.vector.memset(any_out[:, :], 0.0).then_inc(acc_ready, 1)
            with dve.Else():
                with dve.Fori(0, ET) as t:
                    dve.wait_ge(g_ew, t + 1)
                    dve.wait_ge(g_row, t * 16 + 16)
                    multiply(prods[:, 0], ew_ps[0], 0, 1).then_inc(g_prod, 1)
                    nc.vector.tensor_copy(slow_dst[:, :], dst_f[:, bass.ds(t, 1)]).then_inc(g_chain, 1)
                    with dve.Fori(0, NT) as w:
                        done = t * NT + w
                        dve.wait_ge(g_chain, done + t + 1)
                        for k in range(4):
                            last = nc.vector.tensor_scalar(slow_sel[:, k, :], iota[:, :], slow_dst[:, 0:1],
                                                           y_sb[:, bass.ds(t, 1), k], ALU.is_equal, ALU.mult)
                        last.then_inc(g_sel, 1)
                        dve.wait_ge(g_sel, done + 1)
                        nc.vector.tensor_scalar(slow_dst[:, :], slow_dst[:, :], float(-P), None, ALU.add).then_inc(g_chain, 1)
                        dve.wait_ge(g_msg, done + 1)
                        win = acc[:, 0:4, bass.ds(w * P, P)]
                        nc.vector.tensor_tensor(win, win, bank[6][:, :].rearrange("p (g n) -> p g n", g=4), ALU.add)
                        win = acc[:, 4, bass.ds(w * P, P)]
                        nc.vector.tensor_tensor(win, win, bank[7][:, 0:P], ALU.add).then_inc(g_add, 1)
                        dve.wait_ge(g_add, done + 1)
                nc.vector.memset(any_out[:, :], 0.0).then_inc(acc_ready, 1)

            for t in range(NT):
                dve.wait_ge(fin_mm, t + 1)
                if t >= 4:
                    dve.wait_ge(o_out[t % 4], 16 * (t // 4))
                nc.vector.scalar_tensor_tensor(o_sb[:, t % 4, :], bank[t % 4][:, 0:WIDTH], c_o[:, t:t + 1], x_sb[:, t, :],
                                               ALU.mult, ALU.add).then_inc(fin_done, 1)


MESSAGES = ((0, P, slice(0, 1), slice(0, 1)), (4, P, slice(1, 4, 2), slice(1, 5, 3)), (5, P, slice(2, 3), slice(2, 3)),
            (2, P, slice(0, 1), slice(3, 4)), (8, MUL, slice(3, 4), slice(4, 5)))
GENERAL = ((0, P, 0, 0), (4, P, 1, 1), (4, P, 3, 4), (5, P, 2, 2), (2, P, 0, 3), (8, MUL, 3, 4))


def at_pair(i, q):
    return (i - 1, q + 8) if q < 0 else (i, q)


def kernel(x, src, dst, edge_attr_10, edge_attr_4, node_vec1, L0_gnn_W_li0, L0_gnn_W_li1, L0_gnn_W_lm0, L0_gnn_W_lm1,
           L0_gnn_W_mlp1, L0_gnn_W_mlp2, L0_gnn_W_lo0, L0_gnn_W_lo1):
    import numpy as np
    import concourse.bacc as bacc
    from concourse.bass_utils import run_bass_kernel_spmd

    def padded(a, rows):
        out = np.zeros((rows,) + a.shape[1:], a.dtype)
        out[:a.shape[0]] = a
        return out

    x, src, dst = np.asarray(x), np.asarray(src), np.asarray(dst)
    nodes = np.concatenate([x[:, :MUL], x[:, MUL:].reshape(NODES, MUL, 3).transpose(0, 2, 1).reshape(NODES, 3 * MUL)], axis=1)
    arrays = {
        "in_x": padded(nodes, NODES_PAD),
        "in_src": np.ascontiguousarray(padded(src, EDGES_PAD).reshape(ET, P).T),
        "in_dst": np.ascontiguousarray(padded(dst, EDGES_PAD).reshape(ET, P).T),
        "in_el": np.ascontiguousarray(padded(np.asarray(edge_attr_10), EDGES_PAD).T),
        "in_y": np.ascontiguousarray(padded(np.asarray(edge_attr_4), EDGES_PAD).reshape(ET, P, 4).transpose(1, 0, 2).reshape(P, ET * 4)),
        "in_attr": np.ascontiguousarray(padded(np.asarray(node_vec1), NODES_PAD).reshape(NT, P).T),
        "in_li0": np.asarray(L0_gnn_W_li0), "in_li1": np.asarray(L0_gnn_W_li1),
        "in_lm0": np.asarray(L0_gnn_W_lm0), "in_lm1": np.asarray(L0_gnn_W_lm1),
        "in_mlp1": np.asarray(L0_gnn_W_mlp1), "in_mlp2": np.asarray(L0_gnn_W_mlp2),
        "in_lo0": np.asarray(L0_gnn_W_lo0), "in_lo1": np.asarray(L0_gnn_W_lo1),
    }
    nc = bacc.Bacc("TRN2", target_bir_lowering=False, num_devices=1)
    args = [nc.dram_tensor(n, a.shape, mybir.dt.from_np(a.dtype), kind="ExternalInput").ap() for n, a in arrays.items()]
    out = nc.dram_tensor("out_nodes", (NODES_PAD, WIDTH), mybir.dt.float32, kind="ExternalOutput").ap()
    gnn_layer(nc, *args, out)
    r = run_bass_kernel_spmd(nc, [arrays], core_ids=[0])
    got = np.asarray(r.results[0]["out_nodes"])[:NODES]
    vec = got[:, MUL:].reshape(NODES, 3, MUL).transpose(0, 2, 1).reshape(NODES, 3 * MUL)
    return np.concatenate([got[:, :MUL], vec], axis=1)
```

```python
import math
from contextlib import ExitStack

import concourse.bass as bass
from concourse import mybir

NODES, EDGES, MUL, BASIS, HID = 3125, 53125, 64, 10, 100
P = 128
WIDTH = 4 * MUL
NT = -(-NODES // P)
NODES_PAD = NT * P
BODY = 16
ET = -(-EDGES // (P * BODY)) * BODY
EDGES_PAD = ET * P
ET_FULL = EDGES // P
LAST_EDGES = EDGES - ET_FULL * P
ITERS = ET // BODY
HALF = BODY // 2
WIN = 16
LO = 64
HI = 50
GROUPS = 6
BLOCKS = 6
PARTS = 3
SELS = 6
SLOTS = BODY
XB = 4
LAG = 2
EPS = 1e-5
C_S, C_X = math.sin(math.pi / 8), math.cos(math.pi / 8)


def gnn_layer(nc, x_nodes, src_t, dst_t, el_t, edge_y, attr_t, w_li0, w_li1, w_lm0, w_lm1, w_mlp1, w_mlp2,
              w_lo0, w_lo1, out):
    f32, bf16, i32 = mybir.dt.float32, mybir.dt.bfloat16, mybir.dt.int32
    ALU, ACT, AX = mybir.AluOpType, mybir.ActivationFunctionType, mybir.AxisListType

    ctx = ExitStack()
    with ctx:
        def sb(name, shape, dt=f32):
            return ctx.enter_context(nc.sbuf_tensor(name, shape, dt))

        def sem(name):
            return ctx.enter_context(nc.semaphore(name))

        table = nc.dram_tensor("table", (NODES_PAD, WIDTH), f32, kind="Internal").ap()
        el_parts = nc.dram_tensor("el_parts", (PARTS * BASIS, EDGES_PAD), bf16, kind="Internal").ap()

        ACC = GROUPS * NODES_PAD
        arena = sb("arena", [P, max((LO + HI) * ET // 2, ACC + NT * WIDTH)])
        onehot = arena[:, 0:(LO + HI) * ET // 2].bitcast(bf16).rearrange("p (j t) -> p j t", t=ET)
        acc = arena[:, 0:ACC].rearrange("p (g n) -> p g n", g=GROUPS)
        f_rows = arena[:, ACC:ACC + NT * WIDTH].rearrange("p (t f) -> p t f", t=NT)
        g_rows = arena[:, ACC:ACC + SLOTS * WIDTH].rearrange("p (s f) -> p s f", s=SLOTS)
        GY = ACC + SLOTS * WIDTH
        gy = arena[:, GY:GY + XB * 2 * 3 * MUL].rearrange("p (s t m u) -> p s t m u", s=XB, t=2, m=3)

        room = sb("room", [P, NT * WIDTH])
        taken = [0]

        def view(free, dt=f32):
            n = free * (2 if dt == bf16 else 4) // 4
            at = taken[0]
            taken[0] += n
            assert taken[0] <= NT * WIDTH
            v = room[:, at:at + n]
            return v if dt == f32 else v.bitcast(dt)

        EL = BASIS * EDGES_PAD // P
        el_flat = view(EL)
        hi_i, lo_i = view(ET, i32), view(ET, i32)
        hi_b, lo_b = view(ET, bf16), view(ET, bf16)
        hT = room[:, :].rearrange("p (t f) -> p t f", t=NT)
        taken[0] = 0
        prods = view(XB * 2 * BLOCKS * MUL).rearrange("p (s t b u) -> p s t b u", s=XB, t=2, b=BLOCKS)
        sel = view(2 * HALF * SELS * WIN).rearrange("p (h t k j) -> p h t k j", h=2, t=HALF, k=SELS)
        hid = view(2 * 4 * P)[0:HID, :].rearrange("p (s e) -> p s e", s=2)
        slow_sel = view(5 * P).rearrange("p (k j) -> p k j", k=5)
        o_sb = room[:, 0:4 * WIDTH].rearrange("p (s f) -> p s f", s=4)
        el_bits = sb("el_bits", [P, 2, EL], bf16)
        x_sb = sb("x_sb", [P, NT, WIDTH])
        stats = sb("stats", [P, NT, 6])
        mean_var = sb("mean_var", [P, NT, 2])
        std = sb("std", [P, NT])
        rstd = sb("rstd", [P, NT])
        shift = sb("shift", [P, NT])
        normed = sb("normed", [P, 4, WIDTH])
        ident = sb("ident", [P, P])
        ones = sb("ones", [P, P])
        iota = sb("iota", [P, P])
        attr = sb("attr", [P, NT])
        deg = sb("deg", [P, NT])
        sdeg = sb("sdeg", [P, NT])
        isq = sb("isq", [P, NT])
        c_f = sb("c_f", [P, NT])
        c_m = sb("c_m", [P, NT])
        c_o = sb("c_o", [P, NT])
        a8 = sb("a8", [P, NT])
        src_i = sb("src_i", [P, ET], i32)
        dst_i = sb("dst_i", [P, ET], i32)
        dst_f = sb("dst_f", [P, ET])
        rel = sb("rel", [P, ET])
        below = sb("below", [P, ET])
        outside = sb("outside", [P, ET])
        any_out = sb("any_out", [P, 1])
        flag = sb("flag", [1, 1], i32)
        bases = sb("bases", [1, ET + 2 * LAG + BODY], i32)
        y_sb = sb("y_sb", [P, ET, 4])
        y_flat = y_sb[:, :, :].rearrange("p t k -> p (t k)")
        w_in_a = sb("w_in_a", [P, 2, P])
        w_in_b = sb("w_in_b", [P, 2, P])
        lo_w = sb("lo_w", [P, 3, P])
        twice = sb("twice", [LO, 2 * LO])
        hist = sb("hist", [LO, HI])
        w1 = sb("w1", [BASIS, HID])
        w2_raw = sb("w2_raw", [HID, WIDTH])
        w2 = sb("w2", [HID, WIDTH])
        idx = sb("idx", [P, 2, HALF], i32)
        KEL = PARTS * PARTS * BASIS
        el = sb("el", [KEL, 2, HALF * P], bf16)
        w1_parts = sb("w1_parts", [BASIS, PARTS, HID], bf16)
        w1_rest = sb("w1_rest", [BASIS, 1, HID])
        w1_stack = sb("w1_stack", [KEL, HID], bf16)
        slow_dst = sb("slow_dst", [P, 1])

        bank = [ctx.enter_context(nc.psum_tensor(f"bank{i}", [P, 512], f32)) for i in range(8)]
        hist_ps = bank[0][0:LO, 0:HI]
        deg_ps = bank[0][:, 128:128 + HI]
        out_ps = bank[0][0:1, 64:65]
        base_ps = bank[1][:, 0:ET]
        hid_ps = bank[0:2]
        ew_ps = [b[:, :].rearrange("p (t f) -> p t f", t=2) for b in bank[2:6]]
        def fm_view(t):
            return bank[2 + t % 4][:, :].rearrange("p (h n f) -> p h n f", h=2, n=2)

        msg_ps = [b[:, 0:4 * SELS * WIN].rearrange("p (t g j) -> p t g j", t=2, g=2 * SELS) for b in bank[6:8]]

        zeroed = sem("zeroed")
        consts = sem("consts")
        dst_in, src_in, y_in, attr_in, w_in = (sem(n) for n in ("dst_in", "src_in", "y_in", "attr_in", "w_in"))
        x_in = [sem(f"x_in{c}") for c in range(5)]
        v_step = sem("v_step")
        base_mm, hist_mm, out_mm = sem("base_mm"), sem("hist_mm"), sem("out_mm")
        hist_ready, deg_mm = sem("hist_ready"), sem("deg_mm")
        dstf_ready, onehots_ready, anyout_ready = sem("dstf_ready"), sem("onehots_ready"), sem("anyout_ready")
        stats_ready, std_ready, normed_ready = sem("stats_ready"), sem("std_ready"), sem("normed_ready")
        trans_done, hT_ready, fm_done, f_scaled = sem("trans_done"), sem("hT_ready"), sem("fm_done"), sem("f_scaled")
        res_done = sem("res_done")
        deg_ready, sdeg_ready, cf_ready = sem("deg_ready"), sem("sdeg_ready"), sem("cf_ready")
        flag_ready, w2_ready, acc_zeroed, bases_ready = (sem(n) for n in ("flag_ready", "w2_ready", "acc_zeroed", "bases_ready"))
        table_out = sem("table_out")
        acc_ready = sem("acc_ready")
        fin_mm, fin_done = sem("fin_mm"), sem("fin_done")
        o_out = [sem(f"o_out{i}") for i in range(4)]
        el_stored = [sem(f"el_stored{n}") for n in range(PARTS)]
        el_in, el_split, el_rest, w1_split, w1_moved = (sem(n) for n in (
            "el_in", "el_split", "el_rest", "w1_split", "w1_moved"))
        el_ready = [sem(f"el_ready{b}") for b in range(2)]
        gathered = [sem(f"gathered{s}") for s in range(SLOTS)]
        idx_ready, hid_mm, silu_done, ew_mm = sem("idx_ready"), sem("hid_mm"), sem("silu_done"), sem("ew_mm")
        prod_done, msg_mm, add_done, oh_done, sel_ready = (sem(n) for n in ("prod_done", "msg_mm", "add_done", "oh_done", "sel_ready"))
        gy_ready, q_step, g_gy, g_q = sem("gy_ready"), sem("q_step"), sem("g_gy"), sem("g_q")
        g_el, g_idx, g_row, g_hid, g_silu, g_ew, g_prod, g_sel, g_msg, g_add, g_chain = (
            sem("g_" + n) for n in ("el", "idx", "row", "hid", "silu", "ew", "prod", "sel", "msg", "add", "chain"))

        block = ctx.enter_context(nc.Block())
        NW = 16

        def flagged(eng):
            eng.wait_ge(flag_ready, 1)
            return eng.value_load(flag[0:1, 0:1], min_val=0, max_val=1)

        @block.sync
        def _(sp):
            sp.dma_start(dst_i[:, :], dst_t).then_inc(dst_in, 16)
            sp.dma_start(el_flat, el_t.rearrange("c e -> (c e)").rearrange("(p x) -> p x", p=P)).then_inc(el_in, 16)
            x_v = x_nodes.rearrange("(t p) f -> p t f", p=P)
            for c in range(5):
                sp.dma_start(x_sb[:, 5 * c:5 * c + 5, :], x_v[:, 5 * c:5 * c + 5, :]).then_inc(x_in[c], 16)
            sp.dma_start(src_i[:, :], src_t).then_inc(src_in, 16)
            sp.dma_start(y_sb[:, :, :], edge_y.rearrange("p (t k) -> p t k", k=4)).then_inc(y_in, 16)
            for n in range(PARTS):
                rows = el_parts[n * BASIS:(n + 1) * BASIS, :].rearrange("c e -> (c e)").rearrange("(p x) -> p x", p=P)
                sp.wait_ge(el_split, n + 1)
                sp.dma_start(rows, el_bits[:, n % 2, :]).then_inc(el_stored[n], 16)
            sp.wait_ge(w1_split, PARTS)
            for j in range(PARTS):
                for i in range(PARTS):
                    row = (j * PARTS + i) * BASIS
                    sp.dma_start(w1_stack[row:row + BASIS, :], w1_parts[:, j, :]).then_inc(w1_moved, 16)
            t_v = table.rearrange("(t p) f -> p t f", p=P)
            for c in range(5):
                sp.wait_ge(f_scaled, 5 * c + 5)
                sp.dma_start(t_v[:, 5 * c:5 * c + 5, :], f_rows[:, 5 * c:5 * c + 5, :]).then_inc(table_out, 16)

            def load_el(i, b):
                load_rows(el[:, b, :], (i * 2 + b) * HALF * P, HALF * P, el_ready[b])

            def load_rows(to, e0, n, ready):
                for j in range(PARTS):
                    sp.dma_start(to[j * PARTS * BASIS:(j + 1) * PARTS * BASIS, :], el_parts[:, bass.ds(e0, n)]).then_inc(ready, 16)

            fl = flagged(sp)
            for n in range(PARTS):
                sp.wait_ge(el_stored[n], 16)
            with sp.If(fl == 0):
                load_el(0, 0)
                load_el(0, 1)
                with sp.Fori(1, ITERS) as i:
                    for b in range(2):
                        sp.wait_ge(hid_mm, i * 4 + (2 * b - 2))
                        load_el(i, b)
            with sp.Else():
                load_rows(el[:, 0, 0:P], 0, P, g_el)
                with sp.Fori(1, ET) as t:
                    sp.wait_ge(g_hid, t)
                    load_rows(el[:, 0, 0:P], t * P, P, g_el)

            o_v = out.rearrange("(t p) f -> t p f", p=P)
            for t in range(NT):
                sp.wait_ge(fin_done, t + 1)
                sp.dma_start(o_v[t, :, :], o_sb[:, t % 4, :]).then_inc(o_out[t % 4], 16)
            for s in range(4):
                sp.wait_ge(o_out[s], 16 * len(range(s, NT, 4)))

        @block.gpsimd
        def _(pool):
            for w in (w_in_a, w_in_b):
                nc.gpsimd.memset(w[:, :, :], 0.0).then_inc(zeroed, 1)
            nc.gpsimd.memset(lo_w[:, :, :], 0.0).then_inc(zeroed, 1)
            nc.gpsimd.memset(ones[:, :], 1.0).then_inc(consts, 1)
            nc.gpsimd.iota(iota[:, :], pattern=[[1, P]], base=0, channel_multiplier=0,
                           allow_small_or_imprecise_dtypes=True).then_inc(consts, 1)
            nc.gpsimd.memset(ident[:, :], 0.0).then_inc(consts, 1)
            pool.wait_ge(consts, 3)
            nc.gpsimd.affine_select(out=ident[:, :], in_=ident[:, :], compare_op=ALU.not_equal, fill=1.0, base=0,
                                    pattern=[[-1, P]], channel_multiplier=1).then_inc(consts, 1)
            pool.wait_ge(consts, 4)
            for h in range(2):
                nc.gpsimd.tensor_copy(twice[:, h * LO:h * LO + LO], ident[0:LO, 0:LO]).then_inc(consts, 1)
            pool.wait_ge(el_split, 1)
            nc.gpsimd.tensor_tensor(el_flat, el_flat, el_bits[:, 0, :], ALU.subtract).then_inc(el_rest, 1)
            pool.wait_ge(el_split, 2)
            pool.wait_ge(el_stored[0], 16)
            nc.gpsimd.tensor_tensor(el_bits[:, 0, :], el_flat, el_bits[:, 1, :], ALU.subtract).then_inc(el_split, 1)
            pool.wait_ge(hist_mm, 1)
            nc.gpsimd.memset(acc, 0.0).then_inc(acc_zeroed, 1)
            pool.wait_ge(src_in, 16)
            fl = flagged(pool)

            counts = [pool.alloc_register(f"count_{n}") for n in range(2)]

            def value(v, n):
                if isinstance(v, int):
                    return v
                pool.reg_mov(counts[n], v)
                return counts[n]

            def copy_idx(i, b):
                if not (isinstance(i, int) and i == 0):
                    pool.wait_ge(prod_done, i * 8 + (4 * b - 4))
                nc.gpsimd.tensor_copy(idx[:, b, :], src_i[:, bass.ds((i * 2 + b) * HALF, HALF)]).then_inc(idx_ready, 1)

            def body(i, first):
                for k in range(BODY):
                    b = k // HALF
                    if k % HALF == 0:
                        copy_idx(i, b)
                    copied = value(i * 2 + (b + 1), 0)
                    used = value(i * (BODY // 2) + ((k - SLOTS) // 2 + 1), 1)
                    pool.wait_ge(table_out, 5 * 16)
                    if k % HALF == 0:
                        pool.wait_ge(idx_ready, copied)
                    if not (first and k < SLOTS):
                        pool.wait_ge(prod_done, used)
                    nc.gpsimd.indirect_dma_start(
                        g_rows[:, k % SLOTS, :], None, table[:, :],
                        bass.IndirectOffsetOnAxis(idx[:, b, k % HALF:k % HALF + 1], 0)).then_inc(gathered[k % SLOTS], 16)

            with pool.If(fl == 0):
                body(0, True)
                with pool.Fori(1, ITERS) as i:
                    body(i, False)
            with pool.Else():
                def one_tile(t):
                    if not isinstance(t, int):
                        pool.wait_ge(g_prod, t)
                    nc.gpsimd.tensor_copy(idx[:, 0, 0:1], src_i[:, bass.ds(t, 1)]).then_inc(g_idx, 1)
                    copied = value(t + 1, 0)
                    pool.wait_ge(table_out, 5 * 16)
                    pool.wait_ge(g_idx, copied)
                    nc.gpsimd.indirect_dma_start(g_rows[:, 0, :], None, table[:, :],
                                                 bass.IndirectOffsetOnAxis(idx[:, 0, 0:1], 0)).then_inc(g_row, 16)

                one_tile(0)
                with pool.Fori(1, ET) as t:
                    one_tile(t)

        @block.tensor
        def _(pe):
            pe.wait_ge(consts, 6)
            pe.wait_ge(dstf_ready, 1)
            nc.tensor.matmul(base_ps, ones[0:1, :], dst_f[0:1, :], start=True, stop=True).then_inc(base_mm, 1)
            pe.wait_ge(onehots_ready, 1)
            for t in range(ET_FULL + 1):
                n = P if t < ET_FULL else LAST_EDGES
                last = nc.tensor.matmul(hist_ps, onehot[0:n, 0:LO, t], onehot[0:n, LO:LO + HI, t],
                                        start=(t == 0), stop=(t == ET_FULL))
            last.then_inc(hist_mm, 1)
            pe.wait_ge(hist_ready, 1)
            nc.tensor.matmul(deg_ps, twice[:, :], hist[:, :], start=True, stop=True).then_inc(deg_mm, 1)
            pe.wait_ge(w_in, NW * 16)

            def transposes(t):
                pe.wait_ge(normed_ready, t + 1)
                if t >= 2:
                    pe.wait_ge(hT_ready, t - 1)
                for h in range(2):
                    last = nc.tensor.transpose(bank[6 + t % 2][:, h * P:h * P + P],
                                               normed[:, t % 4, h * P:h * P + P], ident[:, :])
                last.then_inc(trans_done, 1)

            def project(t):
                pe.wait_ge(hT_ready, t + 1)
                if t >= 4:
                    pe.wait_ge(f_scaled, t - 3)
                    pe.wait_ge(res_done, t - 3)
                for h, w in enumerate((w_in_a, w_in_b)):
                    last = nc.tensor.matmul(bank[2 + t % 4][:, h * WIDTH:(h + 1) * WIDTH], hT[:, t, h * P:h * P + P],
                                            w[:, :, :].rearrange("p n f -> p (n f)"), start=True, stop=True)
                last.then_inc(fm_done, 1)

            pe.wait_ge(anyout_ready, 1)
            nc.tensor.matmul(out_ps, any_out[:, :], ones[:, 0:1], start=True, stop=True).then_inc(out_mm, 1)
            for t in range(NT + 2):
                if t < NT:
                    transposes(t)
                if t >= 2:
                    project(t - 2)

            fl = flagged(pe)
            pe.wait_ge(res_done, NT)
            pe.wait_ge(w2_ready, 1)
            pe.wait_ge(w1_moved, 16 * PARTS * PARTS)

            def hidden(i, c):
                b = c // 2
                if c % 2 == 0:
                    pe.wait_ge(el_ready[b], i * (16 * PARTS) + 16 * PARTS)
                if not (isinstance(i, int) and 4 * i + c < 2):
                    pe.wait_ge(silu_done, i * 4 + (c - 1))
                nc.tensor.matmul(hid_ps[c % 2][0:HID, :], w1_stack[:, :], el[:, b, (c % 2) * 512:(c % 2) * 512 + 512],
                                 start=True, stop=True).then_inc(hid_mm, 1)

            def edge_weights(i, q):
                g = q // 2
                if q % 2 == 0:
                    pe.wait_ge(silu_done, i * 4 + (g + 1))
                if not (isinstance(i, int) and 8 * i + q < 4):
                    pe.wait_ge(prod_done, i * 8 + (q - 3))
                for tt in range(2):
                    e0 = (q % 2) * 2 * P + tt * P
                    last = nc.tensor.matmul(ew_ps[q % 4][:, tt, :], hid[:, g % 2, e0:e0 + P], w2[:, :],
                                            start=True, stop=True)
                last.then_inc(ew_mm, 1)

            def messages(i, q):
                pe.wait_ge(prod_done, i * 8 + (q + 1))
                if q % 4 == 0:
                    pe.wait_ge(sel_ready, i * 2 + (q // 4 + 1))
                if not (isinstance(i, int) and 8 * i + q < 2):
                    pe.wait_ge(add_done, i * 16 + 2 * (q - 1))
                for tt in range(2):
                    T = 2 * q + tt
                    pr = prods[:, q % XB, tt, :, :].rearrange("p b u -> p (b u)")
                    s = sel[:, (T // HALF) % 2, T % HALF, :, :]
                    for block, g in MESSAGES:
                        last = nc.tensor.matmul(msg_ps[q % 2][:, tt, g:g + SELS, :], pr[:, block * MUL:block * MUL + P], s,
                                                start=True, stop=True)
                last.then_inc(msg_mm, 1)

            def body(i):
                for c in range(4):
                    hidden(i, c)
                    for q in (2 * c - 2, 2 * c - 1):
                        if not (isinstance(i, int) and q < 0):
                            edge_weights(*at_pair(i, q))
                        if not (isinstance(i, int) and q < LAG):
                            messages(*at_pair(i, q - LAG))

            with pe.If(fl == 0):
                body(0)
                with pe.Fori(1, ITERS) as i:
                    body(i)
                for q in (6, 7, 8, 9):
                    if q < 8:
                        edge_weights(ITERS - 1, q)
                    messages(ITERS - 1, q - LAG)
            with pe.Else():
                with pe.Fori(0, ET) as t:
                    pe.wait_ge(g_el, t * (16 * PARTS) + 16 * PARTS)
                    nc.tensor.matmul(hid_ps[0][0:HID, 0:P], w1_stack[:, :], el[:, 0, 0:P],
                                     start=True, stop=True).then_inc(g_hid, 1)
                    pe.wait_ge(g_silu, t + 1)
                    nc.tensor.matmul(ew_ps[0][:, 0, :], hid[:, 0, 0:P], w2[:, :], start=True, stop=True).then_inc(g_ew, 1)
                    pe.wait_ge(acc_zeroed, 1)
                    pe.wait_ge(g_prod, t + 1)
                    with pe.Fori(0, NT) as w:
                        pe.wait_ge(g_sel, t * NT + w + 1)
                        pr = prods[:, 0, 0, :, :].rearrange("p b u -> p (b u)")
                        for block, k, g in GENERAL:
                            into = bank[6 + g // 4][:, g % 4 * P:g % 4 * P + P]
                            last = nc.tensor.matmul(into, pr[:, block * MUL:block * MUL + P],
                                                    slow_sel[:, k, :], start=True, stop=True)
                        last.then_inc(g_msg, 1)

            pe.wait_ge(acc_ready, 1)
            for t in range(NT):
                o_ps = bank[t % 4]
                if t >= 4:
                    pe.wait_ge(fin_done, t - 3)
                cols = o_ps[:, 0:WIDTH].rearrange("p (j u) -> p j u", j=4)
                for g in range(2):
                    nc.tensor.matmul(cols[:, 2 * g:2 * g + 2, :], acc[:, 4 + g, t * P:t * P + P],
                                     lo_w[:, g, :].rearrange("p (j u) -> p j u", j=2), start=(g == 0), stop=False)
                nc.tensor.matmul(cols[:, 0, :], acc[:, 0, t * P:t * P + P], lo_w[:, 2, 0:MUL], start=False, stop=False)
                for g in range(1, 4):
                    last = nc.tensor.matmul(cols[:, g, :], acc[:, g, t * P:t * P + P], lo_w[:, 2, MUL:P],
                                            start=False, stop=(g == 3))
                last.then_inc(fin_mm, 1)

        @block.scalar
        def _(act):
            act.dma_start(attr[:, :], attr_t).then_inc(attr_in, 16)
            act.dma_start(w1[:, :], w_mlp1).then_inc(w_in, 16)
            act.dma_start(w2_raw[:, :], w_mlp2).then_inc(w_in, 16)
            act.wait_ge(zeroed, 3)
            A, B = slice(0, MUL), slice(MUL, P)
            for n, (w0, w1_) in enumerate(((w_li0, w_li1), (w_lm0, w_lm1))):
                act.dma_start(w_in_a[A, n, A], w0).then_inc(w_in, 16)
                act.dma_start(w_in_a[B, n, B], w1_).then_inc(w_in, 16)
                act.dma_start(w_in_b[A, n, A], w1_).then_inc(w_in, 16)
                act.dma_start(w_in_b[B, n, B], w1_).then_inc(w_in, 16)
            act.dma_start(lo_w[A, 0, A], w_lo0[0:MUL, :]).then_inc(w_in, 16)
            act.dma_start(lo_w[B, 0, B], w_lo1[MUL:P, :]).then_inc(w_in, 16)
            act.dma_start(lo_w[A, 1, A], w_lo1[MUL:P, :]).then_inc(w_in, 16)
            act.dma_start(lo_w[B, 1, B], w_lo1[MUL:P, :]).then_inc(w_in, 16)
            act.dma_start(lo_w[A, 2, B], w_lo1[0:MUL, :]).then_inc(w_in, 16)
            act.dma_start(lo_w[B, 2, A], w_lo0[MUL:P, :]).then_inc(w_in, 16)

            act.wait_ge(el_in, 16)
            nc.scalar.activation(el_bits[:, 0, :], el_flat, ACT.Copy).then_inc(el_split, 1)
            act.wait_ge(el_rest, 1)
            nc.scalar.activation(el_bits[:, 1, :], el_flat, ACT.Copy).then_inc(el_split, 1)
            act.wait_ge(stats_ready, 1)
            nc.scalar.activation(std[:, :], mean_var[:, :, 1], ACT.Sqrt).then_inc(std_ready, 1)
            act.wait_ge(deg_ready, 1)
            nc.scalar.activation(sdeg[:, :], deg[:, :], ACT.Sqrt).then_inc(sdeg_ready, 1)
            act.wait_ge(el_split, 3)
            act.wait_ge(onehots_ready, 1)
            for t in range(NT + 2):
                if t < NT:
                    act.wait_ge(trans_done, t + 1)
                    nc.scalar.activation(hT[:, t, :], bank[6 + t % 2][:, 0:WIDTH], ACT.Relu).then_inc(hT_ready, 1)
                if t == 1:
                    act.wait_ge(cf_ready, 1)
                if t >= 2:
                    act.wait_ge(fm_done, t - 1)
                    nc.scalar.activation(f_rows[:, t - 2, :].rearrange("p (h f) -> p h f", h=2), fm_view(t - 2)[:, :, 0, :], ACT.Copy,
                                         scale=c_f[:, t - 2:t - 1]).then_inc(f_scaled, 1)

            fl = flagged(act)

            def silu(i, c):
                act.wait_ge(hid_mm, i * 4 + (c + 1))
                if not (isinstance(i, int) and 4 * i + c < 2):
                    act.wait_ge(ew_mm, i * 8 + (2 * c - 2))
                nc.scalar.activation(hid[:, c % 2, :], hid_ps[c % 2][0:HID, :], ACT.Silu,
                                     scale=1.0 / math.sqrt(BASIS)).then_inc(silu_done, 1)

            def scale_rows(out, slot, y):
                for m in range(3):
                    last = nc.scalar.activation(out[:, m, :], g_rows[:, slot, (1 + m) * MUL:(2 + m) * MUL], ACT.Copy,
                                                scale=y(1 + m))
                return last

            def scaled_rows(i, q):
                if not (isinstance(i, int) and 8 * i + q < XB):
                    act.wait_ge(prod_done, i * 8 + (q + 1 - XB))
                for tt in range(2):
                    T = 2 * q + tt
                    act.wait_ge(gathered[T % SLOTS], i * (16 * BODY // SLOTS) + 16 * (T // SLOTS + 1))
                    last = scale_rows(gy[:, q % XB, tt], T % SLOTS, lambda k: y_at(i, T, k))
                last.then_inc(gy_ready, 1)

            def y_at(i, T, k):
                if isinstance(i, int):
                    return y_sb[:, i * BODY + T, k:k + 1]
                return y_flat[:, bass.ds((i * BODY + T) * 4 + k, 1)]

            def body(i):
                for c in range(4):
                    silu(i, c)
                    for q in (2 * c, 2 * c + 1):
                        scaled_rows(i, q)

            act.wait_ge(y_in, 16)
            with act.If(fl == 0):
                body(0)
                with act.Fori(1, ITERS) as i:
                    body(i)
            with act.Else():
                def one_tile(t):
                    act.wait_ge(g_hid, t + 1)
                    if not isinstance(t, int):
                        act.wait_ge(g_ew, t)
                        act.wait_ge(g_prod, t)
                    nc.scalar.activation(hid[:, 0, 0:P], hid_ps[0][0:HID, 0:P], ACT.Silu,
                                         scale=1.0 / math.sqrt(BASIS)).then_inc(g_silu, 1)
                    act.wait_ge(g_row, t * 16 + 16)
                    scale_rows(gy[:, 0, 0], 0, lambda k: y_flat[:, bass.ds(t * 4 + k, 1)]).then_inc(g_gy, 1)

                one_tile(0)
                with act.Fori(1, ET) as t:
                    one_tile(t)

        @block.vector
        def _(dve):
            chain = [0]

            def link(ins):
                chain[0] += 1
                ins.then_inc(v_step, 1)
                dve.wait_ge(v_step, chain[0])

            dve.wait_ge(dst_in, 16)
            nc.vector.tensor_copy(dst_f[:, :], dst_i[:, :]).then_inc(dstf_ready, 1)
            nc.vector.tensor_scalar(hi_i, dst_i[:, :], 6, None, ALU.arith_shift_right)
            link(nc.vector.tensor_scalar(lo_i, dst_i[:, :], LO - 1, None, ALU.bitwise_and))
            nc.vector.tensor_copy(lo_b, lo_i)
            link(nc.vector.tensor_copy(hi_b, hi_i))
            for j in range(LO):
                nc.vector.tensor_scalar(onehot[:, j, :], lo_b, float(j), None, ALU.is_equal)
            for j in range(HI):
                last = nc.vector.tensor_scalar(onehot[:, LO + j, :], hi_b, float(j), None, ALU.is_equal)
            last.then_inc(onehots_ready, 1)

            for t in range(NT):
                if t % 5 == 0:
                    dve.wait_ge(x_in[t // 5], 16)
                last = nc.vector.bn_stats(stats[:, t, :], x_sb[:, t, :])
            link(last)
            dve.wait_ge(w_in, NW * 16)
            nc.vector.tensor_copy(w1_parts[:, 0, :], w1[:, :]).then_inc(w1_split, 1)
            dve.wait_ge(w1_split, 1)
            link(nc.vector.tensor_tensor(w1_rest[:, 0, :], w1[:, :], w1_parts[:, 0, :], ALU.subtract))
            nc.vector.tensor_copy(w1_parts[:, 1, :], w1_rest[:, 0, :]).then_inc(w1_split, 1)
            dve.wait_ge(w1_split, 2)
            nc.vector.tensor_tensor(w1_parts[:, 2, :], w1_rest[:, 0, :], w1_parts[:, 1, :], ALU.subtract).then_inc(w1_split, 1)
            for t in range(NT):
                last = nc.vector.bn_aggr(mean_var[:, t, :], stats[:, t, :])
            link(last)
            nc.vector.tensor_scalar(mean_var[:, :, 1], mean_var[:, :, 1], EPS, None, ALU.add).then_inc(stats_ready, 1)
            dve.wait_ge(std_ready, 1)
            link(nc.vector.reciprocal(rstd[:, :], std[:, :]))
            link(nc.vector.scalar_tensor_tensor(shift[:, :], mean_var[:, :, 0], -1.0, rstd[:, :], ALU.mult, ALU.mult))

            def normalise(t):
                if t >= 4:
                    dve.wait_ge(trans_done, t - 3)
                nc.vector.tensor_scalar(normed[:, t % 4, :], x_sb[:, t, :], rstd[:, t:t + 1], shift[:, t:t + 1],
                                        ALU.mult, ALU.add).then_inc(normed_ready, 1)

            for t in range(4):
                normalise(t)

            link(nc.vector.memset(deg[:, :], 1.0))
            dve.wait_ge(hist_mm, 1)
            nc.vector.tensor_copy(hist[:, :], hist_ps).then_inc(hist_ready, 1)
            dve.wait_ge(deg_mm, 1)
            pairs = deg_ps.rearrange("p (t r) -> p t r", r=2)
            nc.vector.tensor_scalar(deg[0:MUL, 0:NT], pairs[0:MUL, 0:NT, 0], 1.0, None, ALU.max)
            nc.vector.tensor_scalar(deg[MUL:P, 0:NT], pairs[MUL:P, 0:NT, 1], 1.0, None, ALU.max).then_inc(deg_ready, 1)
            dve.wait_ge(attr_in, 16)
            dve.wait_ge(sdeg_ready, 1)
            nc.vector.tensor_scalar(a8[:, :], attr[:, :], 1.0 / math.sqrt(MUL), None, ALU.mult)
            link(nc.vector.reciprocal(isq[:, :], sdeg[:, :]))
            nc.vector.tensor_tensor(c_f[:, :], a8[:, :], isq[:, :], ALU.mult).then_inc(cf_ready, 1)
            nc.vector.tensor_scalar(c_m[:, :], a8[:, :], C_S, None, ALU.mult)
            dve.wait_ge(cf_ready, 1)
            link(nc.vector.tensor_scalar(c_o[:, :], c_f[:, :], C_X * math.sqrt(MUL) / math.sqrt(2 * MUL), None, ALU.mult))

            dve.wait_ge(base_mm, 1)
            link(nc.vector.tensor_tensor(rel[:, :], dst_f[:, :], base_ps, ALU.subtract))
            nc.vector.memset(outside[:, :], 0.0)
            link(nc.vector.tensor_scalar(below[:, :], rel[:, :], 0.0, None, ALU.is_lt))
            for n, cols in ((P, slice(0, ET_FULL)), (LAST_EDGES, slice(ET_FULL, ET_FULL + 1))):
                last = nc.vector.scalar_tensor_tensor(outside[0:n, cols], rel[0:n, cols], WIN - 0.5, below[0:n, cols],
                                                      ALU.is_gt, ALU.add)
            link(last)
            nc.vector.reduce_max(any_out[:, :], outside[:, :], AX.X).then_inc(anyout_ready, 1)
            link(nc.vector.memset(bases[:, :], 0))
            nc.vector.tensor_copy(bases[0:1, 2 * LAG:2 * LAG + ET], dst_i[0:1, :]).then_inc(bases_ready, 1)

            dve.wait_ge(w_in, NW * 16)
            k = 1.0 / math.sqrt(HID)
            for n, (o, s) in enumerate(((0, k), (2, k), (3, k), (1, k / math.sqrt(3.0)))):
                last = nc.vector.tensor_scalar(w2[:, n * MUL:(n + 1) * MUL], w2_raw[:, o * MUL:(o + 1) * MUL], s, None, ALU.mult)
            last.then_inc(w2_ready, 1)
            dve.wait_ge(out_mm, 1)
            nc.vector.tensor_scalar(flag[:, :], out_ps, 1.0, None, ALU.min).then_inc(flag_ready, 1)

            for t in range(4, NT + 7):
                if t < NT:
                    normalise(t)
                if t >= 7:
                    dve.wait_ge(f_scaled, t - 6)
                    half = x_sb[:, t - 7, :].rearrange("p (h f) -> p h f", h=2)
                    nc.vector.scalar_tensor_tensor(half, fm_view(t - 7)[:, :, 1, :], c_m[:, t - 7:t - 6], half,
                                                   ALU.mult, ALU.add).then_inc(res_done, 1)

            fl = flagged(dve)
            dve.wait_ge(y_in, 16)
            dve.wait_ge(consts, 4)
            dve.wait_ge(acc_zeroed, 1)
            dve.wait_ge(bases_ready, 1)
            link(nc.vector.memset(sel[:, :, :, SELS - 1, :], 0.0))

            def select(i, b):
                T0 = (i * 2 + b) * HALF
                if not (isinstance(i, int) and i == 0):
                    dve.wait_ge(msg_mm, i * 8 + 4 * (b - 1))
                n = [P, HALF, WIN]
                one = sel[:, b, :, 1, :]
                nc.vector.tensor_tensor(one, iota[:, 0:WIN].unsqueeze(1).broadcast_to(n),
                                        rel[:, bass.ds(T0, HALF)].unsqueeze(2).broadcast_to(n),
                                        ALU.is_equal).then_inc(oh_done, 1)
                dve.wait_ge(oh_done, i * 2 + (b + 1))
                y = y_sb[:, bass.ds(T0, HALF), :]
                nc.vector.tensor_tensor(sel[:, b, :, 0, :], one, y[:, :, 0].unsqueeze(2).broadcast_to(n), ALU.mult)
                n = [P, HALF, 3, WIN]
                nc.vector.tensor_tensor(sel[:, b, :, 2:5, :], one.unsqueeze(2).broadcast_to(n),
                                        y[:, :, 1:4].unsqueeze(3).broadcast_to(n), ALU.mult).then_inc(sel_ready, 1)

            def products(i, q, meanwhile):
                dve.wait_ge(ew_mm, i * 8 + (q + 1))
                for s in ((2 * q) % SLOTS, (2 * q + 1) % SLOTS):
                    dve.wait_ge(gathered[s], i * (16 * BODY // SLOTS) + 16 * (2 * q // SLOTS + 1))
                if not (isinstance(i, int) and 8 * i + q < XB):
                    dve.wait_ge(msg_mm, i * 8 + (q + 1 - XB))
                dve.wait_ge(gy_ready, i * 8 + (q + 1))
                multiply(prods[:, q % XB], ew_ps[q % 4], gy[:, q % XB], (2 * q) % SLOTS, 2, q_step, i * 16 + 2 * q,
                         meanwhile).then_inc(prod_done, 1)

            def multiply(pr, ew, gy_, s0, tiles, step, steps, meanwhile=lambda n: None):
                dot = gy_[:, 0:tiles, 0, :]
                nc.vector.tensor_tensor(dot, dot, gy_[:, 0:tiles, 1, :], ALU.add).then_inc(step, 1)
                g0 = g_rows[:, s0:s0 + tiles, 0:MUL]
                n = [P, tiles, 2, MUL]
                nc.vector.tensor_tensor(pr[:, 0:tiles, 0:5:4, :], ew[:, 0:tiles, 0:2 * MUL].rearrange("p t (b u) -> p t b u", b=2),
                                        g0.unsqueeze(2).broadcast_to(n), ALU.mult)
                meanwhile(0)
                dve.wait_ge(step, steps + 1)
                nc.vector.tensor_tensor(dot, dot, gy_[:, 0:tiles, 2, :], ALU.add).then_inc(step, 1)
                g1 = g_rows[:, s0:s0 + tiles, MUL:].rearrange("p t (m u) -> p t m u", m=3)
                n = [P, tiles, 3, MUL]
                nc.vector.tensor_tensor(pr[:, 0:tiles, 1:4, :], ew[:, 0:tiles, 2 * MUL:3 * MUL].unsqueeze(2).broadcast_to(n),
                                        g1, ALU.mult)
                meanwhile(1)
                dve.wait_ge(step, steps + 2)
                return nc.vector.tensor_tensor(pr[:, 0:tiles, 5, :], ew[:, 0:tiles, 3 * MUL:], dot, ALU.mult)

            def add(i, q, tt, base):
                if tt == 0:
                    dve.wait_ge(msg_mm, i * 8 + (q + 1))
                T = 2 * q + tt
                if not (isinstance(i, int) and 16 * i + T < 1):
                    dve.wait_ge(add_done, i * 16 + T)
                win = acc[:, :, bass.ds(base, WIN)]
                nc.vector.tensor_tensor(win, win, msg_ps[q % 2][:, tt, 1:1 + GROUPS, :], ALU.add).then_inc(add_done, 1)

            base_regs = [dve.alloc_register(f"base_{k}") for k in range(BODY)]

            def load_bases(at, n, r=0):
                regs = base_regs[r:r + n]
                dve.load(regs, bases[0:1, at if isinstance(at, slice) else bass.ds(at, n)])
                return [dve.snap(r, min_val=0, max_val=NODES - 1) for r in regs]

            def body(i):
                base = []
                for q in range(8):
                    if q % 4 == 0:
                        select(i, q // 4)
                    if q % 2 == 0:
                        base += load_bases(i * BODY + 2 * q, 4, 2 * q)
                    late = not (isinstance(i, int) and q < LAG)
                    products(i, q, lambda tt: late and add(*at_pair(i, q - LAG), tt, base[2 * q + tt]))

            with dve.If(fl == 0):
                body(0)
                with dve.Fori(1, ITERS) as i:
                    body(i)
                base = load_bases(ITERS * BODY, 2 * LAG)
                for q in range(LAG):
                    for tt in range(2):
                        add(ITERS - 1, 8 - LAG + q, tt, base[2 * q + tt])
                dve.wait_ge(add_done, ET)
                nc.vector.memset(any_out[:, :], 0.0).then_inc(acc_ready, 1)
            with dve.Else():
                with dve.Fori(0, ET) as t:
                    dve.wait_ge(g_ew, t + 1)
                    dve.wait_ge(g_row, t * 16 + 16)
                    dve.wait_ge(g_gy, t + 1)
                    multiply(prods[:, 0], ew_ps[0], gy[:, 0], 0, 1, g_q, t * 2).then_inc(g_prod, 1)
                    nc.vector.tensor_copy(slow_dst[:, :], dst_f[:, bass.ds(t, 1)]).then_inc(g_chain, 1)
                    with dve.Fori(0, NT) as w:
                        done = t * NT + w
                        dve.wait_ge(g_chain, done + t + 1)
                        nc.vector.tensor_scalar(slow_sel[:, 1, :], iota[:, :], slow_dst[:, 0:1], None, ALU.is_equal)
                        for k in range(4):
                            last = nc.vector.tensor_scalar(slow_sel[:, k + min(k, 1), :], iota[:, :], slow_dst[:, 0:1],
                                                           y_sb[:, bass.ds(t, 1), k], ALU.is_equal, ALU.mult)
                        last.then_inc(g_sel, 1)
                        dve.wait_ge(g_sel, done + 1)
                        nc.vector.tensor_scalar(slow_dst[:, :], slow_dst[:, :], float(-P), None, ALU.add).then_inc(g_chain, 1)
                        dve.wait_ge(g_msg, done + 1)
                        win = acc[:, 0:4, bass.ds(w * P, P)]
                        nc.vector.tensor_tensor(win, win, bank[6][:, :].rearrange("p (g n) -> p g n", g=4), ALU.add)
                        win = acc[:, 4:6, bass.ds(w * P, P)]
                        nc.vector.tensor_tensor(win, win, bank[7][:, 0:2 * P].rearrange("p (g n) -> p g n", g=2), ALU.add).then_inc(g_add, 1)
                        dve.wait_ge(g_add, done + 1)
                nc.vector.memset(any_out[:, :], 0.0).then_inc(acc_ready, 1)

            for t in range(NT):
                dve.wait_ge(fin_mm, t + 1)
                if t >= 4:
                    dve.wait_ge(o_out[t % 4], 16 * (t // 4))
                nc.vector.scalar_tensor_tensor(o_sb[:, t % 4, :], bank[t % 4][:, 0:WIDTH], c_o[:, t:t + 1], x_sb[:, t, :],
                                               ALU.mult, ALU.add).then_inc(fin_done, 1)


MESSAGES = ((4, 0), (0, 5), (2, 6))
GENERAL = ((4, 1, 0), (4, 2, 1), (4, 3, 2), (4, 4, 3), (0, 0, 4), (2, 0, 5))


def at_pair(i, q):
    return (i - 1, q + 8) if q < 0 else (i, q)


def kernel(x, src, dst, edge_attr_10, edge_attr_4, node_vec1, L0_gnn_W_li0, L0_gnn_W_li1, L0_gnn_W_lm0, L0_gnn_W_lm1,
           L0_gnn_W_mlp1, L0_gnn_W_mlp2, L0_gnn_W_lo0, L0_gnn_W_lo1):
    import numpy as np
    import concourse.bacc as bacc
    from concourse.bass_utils import run_bass_kernel_spmd

    def padded(a, rows):
        out = np.zeros((rows,) + a.shape[1:], a.dtype)
        out[:a.shape[0]] = a
        return out

    x, src, dst = np.asarray(x), np.asarray(src), np.asarray(dst)
    nodes = np.concatenate([x[:, :MUL], x[:, MUL:].reshape(NODES, MUL, 3).transpose(0, 2, 1).reshape(NODES, 3 * MUL)], axis=1)
    arrays = {
        "in_x": padded(nodes, NODES_PAD),
        "in_src": np.ascontiguousarray(padded(src, EDGES_PAD).reshape(ET, P).T),
        "in_dst": np.ascontiguousarray(padded(dst, EDGES_PAD).reshape(ET, P).T),
        "in_el": np.ascontiguousarray(padded(np.asarray(edge_attr_10), EDGES_PAD).T),
        "in_y": np.ascontiguousarray(padded(np.asarray(edge_attr_4), EDGES_PAD).reshape(ET, P, 4).transpose(1, 0, 2).reshape(P, ET * 4)),
        "in_attr": np.ascontiguousarray(padded(np.asarray(node_vec1), NODES_PAD).reshape(NT, P).T),
        "in_li0": np.asarray(L0_gnn_W_li0), "in_li1": np.asarray(L0_gnn_W_li1),
        "in_lm0": np.asarray(L0_gnn_W_lm0), "in_lm1": np.asarray(L0_gnn_W_lm1),
        "in_mlp1": np.asarray(L0_gnn_W_mlp1), "in_mlp2": np.asarray(L0_gnn_W_mlp2),
        "in_lo0": np.asarray(L0_gnn_W_lo0), "in_lo1": np.asarray(L0_gnn_W_lo1),
    }
    nc = bacc.Bacc("TRN2", target_bir_lowering=False, num_devices=1)
    args = [nc.dram_tensor(n, a.shape, mybir.dt.from_np(a.dtype), kind="ExternalInput").ap() for n, a in arrays.items()]
    out = nc.dram_tensor("out_nodes", (NODES_PAD, WIDTH), mybir.dt.float32, kind="ExternalOutput").ap()
    gnn_layer(nc, *args, out)
    r = run_bass_kernel_spmd(nc, [arrays], core_ids=[0])
    got = np.asarray(r.results[0]["out_nodes"])[:NODES]
    vec = got[:, MUL:].reshape(NODES, 3, MUL).transpose(0, 2, 1).reshape(NODES, 3 * MUL)
    return np.concatenate([got[:, :MUL], vec], axis=1)
```

```python
import math
from contextlib import ExitStack

import concourse.bass as bass
from concourse import mybir

NODES, EDGES, MUL, BASIS, HID = 3125, 53125, 64, 10, 100
P = 128
WIDTH = 4 * MUL
NT = -(-NODES // P)
NODES_PAD = NT * P
BODY = 16
ET = -(-EDGES // (P * BODY)) * BODY
EDGES_PAD = ET * P
ET_FULL = EDGES // P
LAST_EDGES = EDGES - ET_FULL * P
ITERS = ET // BODY
HALF = BODY // 2
WIN = 16
LO_BITS = 6
LO = 1 << LO_BITS
HI = NODES_PAD // LO
GROUPS = 6
BLOCKS = 6
PARTS = 3
SELS = 6
SLOTS = BODY
XB = 4
LAG = 2
X_CHUNKS = (0, 5, 10, 15, 20, NT)
M_CHUNKS = (0, 2, 6, 12, 18, NT)
T_CHUNKS = (0, 7, 13, 19, 23, NT)
WARM, WARM_END = 5, 3
NEAR = 8
LEAD = 6
LATE = -(-2 * ET // WIDTH)
O_RING = 8
EPS = 1e-5
C_S, C_X = math.sin(math.pi / 8), math.cos(math.pi / 8)


def gnn_layer(nc, x_nodes, src_t, dst_t, el_t, edge_y, attr_t, w_blocks, w_mlp1, w_mlp2, out):
    f32, bf16, i32 = mybir.dt.float32, mybir.dt.bfloat16, mybir.dt.int32
    ALU, ACT, AX = mybir.AluOpType, mybir.ActivationFunctionType, mybir.AxisListType

    ctx = ExitStack()
    with ctx:
        def sb(name, shape, dt=f32):
            return ctx.enter_context(nc.sbuf_tensor(name, shape, dt))

        def sem(name):
            return ctx.enter_context(nc.semaphore(name))

        table = nc.dram_tensor("table", (NODES_PAD, WIDTH), f32, kind="Internal").ap()
        el_parts = nc.dram_tensor("el_parts", (PARTS * BASIS, EDGES_PAD), bf16, kind="Internal").ap()

        ACC = GROUPS * NODES_PAD
        arena = sb("arena", [P, max((LO + HI) * ET // 2, ACC + NT * WIDTH)])
        onehot = arena[:, 0:(LO + HI) * ET // 2].bitcast(bf16).rearrange("p (j t) -> p j t", t=ET)
        acc = arena[:, 0:ACC].rearrange("p (g n) -> p g n", g=GROUPS)
        f_rows = arena[:, ACC:ACC + NT * WIDTH].rearrange("p (t f) -> p t f", t=NT)
        g_rows = arena[:, ACC:ACC + SLOTS * WIDTH].rearrange("p (s f) -> p s f", s=SLOTS)
        GY = ACC + SLOTS * WIDTH
        gy = arena[:, GY:GY + XB * 2 * 3 * MUL].rearrange("p (s t m u) -> p s t m u", s=XB, t=2, m=3)

        room = sb("room", [P, NT * WIDTH])
        taken = [0]

        def view(free, dt=f32):
            n = free * (2 if dt == bf16 else 4) // 4
            at = taken[0]
            taken[0] += n
            assert taken[0] <= NT * WIDTH
            v = room[:, at:at + n]
            return v if dt == f32 else v.bitcast(dt)

        EL = BASIS * EDGES_PAD // P
        el_flat = view(EL)
        parts_i = view(2 * ET, i32).rearrange("p (h t) -> p h t", h=2)
        parts_b = view(2 * ET, bf16).rearrange("p (h t) -> p h t", h=2)
        hT = room[:, :].rearrange("p (t f) -> p t f", t=NT)
        taken[0] = 0
        prods = view(XB * 2 * BLOCKS * MUL).rearrange("p (s t b u) -> p s t b u", s=XB, t=2, b=BLOCKS)
        hid = view(2 * 4 * P)[0:HID, :].rearrange("p (s e) -> p s e", s=2)
        slow_sel = view(5 * P).rearrange("p (k j) -> p k j", k=5)
        o_sb = room[:, 0:O_RING * WIDTH].rearrange("p (s f) -> p s f", s=O_RING)
        el_bits = sb("el_bits", [P, 2, EL], bf16)
        x_sb = sb("x_sb", [P, NT, WIDTH])
        sel = sb("sel", [P, 2, HALF, SELS, WIN])
        stats = sb("stats", [P, NT, 6])
        mean_var = sb("mean_var", [P, NT, 2])
        std = sb("std", [P, NT])
        rstd = sb("rstd", [P, NT])
        shift = sb("shift", [P, NT])
        normed = sb("normed", [P, 4, WIDTH])
        ident = sb("ident", [P, P])
        ones = sb("ones", [P, P])
        iota = sb("iota", [P, P])
        attr = sb("attr", [P, NT])
        deg = sb("deg", [P, NT])
        sdeg = sb("sdeg", [P, NT])
        isq = sb("isq", [P, NT])
        c_f = sb("c_f", [P, NT])
        c_m = sb("c_m", [P, NT])
        c_o = sb("c_o", [P, NT])
        a8 = sb("a8", [P, NT])
        src_i = sb("src_i", [P, ET], i32)
        dst_i = sb("dst_i", [P, ET], i32)
        dst_f = sb("dst_f", [P, ET])
        rel = sb("rel", [P, ET])
        below = f_rows[:, NT - LATE:, :].rearrange("p t f -> p (t f)")[:, 0:ET]
        outside = f_rows[:, NT - LATE:, :].rearrange("p t f -> p (t f)")[:, ET:2 * ET]
        any_out = sb("any_out", [P, 1])
        warm = sb("warm", [1, 1])
        flag = sb("flag", [1, 1], i32)
        bases = sb("bases", [1, ET + 2 * LAG + BODY], i32)
        y_sb = sb("y_sb", [P, ET, 4])
        y_flat = y_sb[:, :, :].rearrange("p t k -> p (t k)")
        blocks = sb("blocks", [P, 8, P])
        w_in, lo_w = blocks[:, 0:4, :], blocks[:, 4:8, :]
        twice = sb("twice", [LO, 2 * LO])
        hist = sb("hist", [LO, HI])
        w1 = sb("w1", [BASIS, HID])
        w2_raw = sb("w2_raw", [HID, WIDTH])
        w2 = sb("w2", [HID, WIDTH])
        idx = sb("idx", [P, 2, HALF], i32)
        KEL = PARTS * PARTS * BASIS
        el = sb("el", [KEL, 2, HALF * P], bf16)
        w1_parts = sb("w1_parts", [BASIS, PARTS, HID], bf16)
        w1_rest = sb("w1_rest", [BASIS, HID])
        w1_stack = sb("w1_stack", [KEL, HID], bf16)
        slow_dst = sb("slow_dst", [P, 1])

        bank = [ctx.enter_context(nc.psum_tensor(f"bank{i}", [P, 512], f32)) for i in range(8)]
        hist_ps = bank[0][0:LO, 0:HI]
        deg_ps = bank[0][:, 128:128 + HI]
        out_ps = bank[0][0:1, 64:65]
        base_ps = bank[1][:, 0:ET]
        hid_ps = bank[0:2]
        ew_ps = [b[:, :].rearrange("p (t f) -> p t f", t=2) for b in bank[2:6]]
        msg_ps = [b[:, 0:4 * SELS * WIN].rearrange("p (t g j) -> p t g j", t=2, g=2 * SELS) for b in bank[6:8]]

        filled, consts = sem("filled"), sem("consts")
        dst_in, src_in, y_in, attr_in, blocks_in, w2_in = (sem(n) for n in (
            "dst_in", "src_in", "y_in", "attr_in", "blocks_in", "w2_in"))
        x_in = [sem(f"x_in{c}") for c in range(5)]
        v_step = sem("v_step")
        base_mm, hist_mm, out_mm = sem("base_mm"), sem("hist_mm"), sem("out_mm")
        hist_ready, deg_mm = sem("hist_ready"), sem("deg_mm")
        dstf_ready, onehots_ready, anyout_ready = sem("dstf_ready"), sem("onehots_ready"), sem("anyout_ready")
        onehots_near = sem("onehots_near")
        stats_ready, std_ready, normed_ready = sem("stats_ready"), sem("std_ready"), sem("normed_ready")
        trans_done, hT_ready, proj_done, f_scaled = sem("trans_done"), sem("hT_ready"), sem("proj_done"), sem("f_scaled")
        res_done = sem("res_done")
        deg_ready, sdeg_ready, cf_ready = sem("deg_ready"), sem("sdeg_ready"), sem("cf_ready")
        flag_ready, w2_ready, acc_zeroed, bases_ready = (sem(n) for n in ("flag_ready", "w2_ready", "acc_zeroed", "bases_ready"))
        table_out = sem("table_out")
        acc_ready = sem("acc_ready")
        moved = [sem(f"moved{c}") for c in range(5)]
        fin_mm, fin_done = sem("fin_mm"), sem("fin_done")
        o_out = [sem(f"o_out{i}") for i in range(O_RING)]
        el_stored = [sem(f"el_stored{n}") for n in range(PARTS)]
        el_in, el_split, el_rest, w1_in, w1_split, w1_rest_ready, w1_moved = (sem(n) for n in (
            "el_in", "el_split", "el_rest", "w1_in", "w1_split", "w1_rest_ready", "w1_moved"))
        el_ready = [sem(f"el_ready{b}") for b in range(2)]
        gathered = [sem(f"gathered{s}") for s in range(SLOTS)]
        idx_ready, hid_mm, silu_done, ew_mm = sem("idx_ready"), sem("hid_mm"), sem("silu_done"), sem("ew_mm")
        prod_done, msg_mm, add_done, oh_done, sel_ready = (sem(n) for n in ("prod_done", "msg_mm", "add_done", "oh_done", "sel_ready"))
        gy_ready, q_step, g_gy, g_q = sem("gy_ready"), sem("q_step"), sem("g_gy"), sem("g_q")
        g_el, g_idx, g_row, g_hid, g_silu, g_ew, g_prod, g_sel, g_msg, g_add, g_chain = (
            sem("g_" + n) for n in ("el", "idx", "row", "hid", "silu", "ew", "prod", "sel", "msg", "add", "chain"))

        block = ctx.enter_context(nc.Block())

        def proj_ps(n):
            return bank[2 + n % 4][:, 0:WIDTH]

        def flagged(eng):
            eng.wait_ge(flag_ready, 1)
            return eng.value_load(flag[0:1, 0:1], min_val=0, max_val=1)

        @block.sync
        def _(sp):
            sp.dma_start(dst_i[:, :], dst_t).then_inc(dst_in, 16)
            sp.dma_start(el_flat, el_t.rearrange("c e -> (c e)").rearrange("(p x) -> p x", p=P)).then_inc(el_in, 16)
            x_v = x_nodes.rearrange("(t p) f -> p t f", p=P)
            for c in range(5):
                tiles = slice(X_CHUNKS[c], X_CHUNKS[c + 1])
                sp.dma_start(x_sb[:, tiles, :], x_v[:, tiles, :]).then_inc(x_in[c], 16)
            sp.dma_start(src_i[:, :], src_t).then_inc(src_in, 16)
            sp.dma_start(y_sb[:, :, :], edge_y.rearrange("p (t k) -> p t k", k=4)).then_inc(y_in, 16)
            for n in range(PARTS):
                if n == PARTS - 1:
                    sp.wait_ge(w1_split, PARTS)
                    for j in range(PARTS):
                        for i in range(PARTS):
                            row = (j * PARTS + i) * BASIS
                            sp.dma_start(w1_stack[row:row + BASIS, :], w1_parts[:, j, :]).then_inc(w1_moved, 16)
                rows = el_parts[n * BASIS:(n + 1) * BASIS, :].rearrange("c e -> (c e)").rearrange("(p x) -> p x", p=P)
                sp.wait_ge(el_split, n + 1)
                sp.dma_start(rows, el_bits[:, n % 2, :]).then_inc(el_stored[n], 16)
            t_v = table.rearrange("(t p) f -> p t f", p=P)
            for c in range(5):
                tiles = slice(T_CHUNKS[c], T_CHUNKS[c + 1])
                sp.wait_ge(f_scaled, T_CHUNKS[c + 1])
                sp.dma_start(t_v[:, tiles, :], f_rows[:, tiles, :]).then_inc(table_out, 16)

            def load_el(i, b):
                load_rows(el[:, b, :], (i * 2 + b) * HALF * P, HALF * P, el_ready[b])

            def load_rows(to, e0, n, ready):
                for j in range(PARTS):
                    sp.dma_start(to[j * PARTS * BASIS:(j + 1) * PARTS * BASIS, :], el_parts[:, bass.ds(e0, n)]).then_inc(ready, 16)

            fl = flagged(sp)
            for n in range(PARTS):
                sp.wait_ge(el_stored[n], 16)
            with sp.If(fl == 0):
                load_el(0, 0)
                load_el(0, 1)
                with sp.Fori(1, ITERS) as i:
                    for b in range(2):
                        sp.wait_ge(hid_mm, i * 4 + (2 * b - 2))
                        load_el(i, b)
            with sp.Else():
                load_rows(el[:, 0, 0:P], 0, P, g_el)
                with sp.Fori(1, ET) as t:
                    sp.wait_ge(g_hid, t)
                    load_rows(el[:, 0, 0:P], t * P, P, g_el)

            sp.wait_ge(acc_ready, 1)
            for c in range(5):
                nodes = slice(M_CHUNKS[c] * P, M_CHUNKS[c + 1] * P)
                sp.dma_start(acc[MUL:P, 2, nodes], acc[0:MUL, 3, nodes]).then_inc(moved[c], 16)

            o_v = out.rearrange("(t p) f -> t p f", p=P)
            for t in range(NT):
                sp.wait_ge(fin_done, t + 1)
                sp.dma_start(o_v[t, :, :], o_sb[:, t % O_RING, :]).then_inc(o_out[t % O_RING], 16)
            for s in range(O_RING):
                sp.wait_ge(o_out[s], 16 * len(range(s, NT, O_RING)))

        @block.gpsimd
        def _(pool):
            nc.gpsimd.memset(ones[:, :], 1.0).then_inc(consts, 1)
            nc.gpsimd.iota(iota[:, :], pattern=[[1, P]], base=0, channel_multiplier=0,
                           allow_small_or_imprecise_dtypes=True).then_inc(consts, 1)
            nc.gpsimd.memset(ident[:, :], 0.0).then_inc(consts, 1)
            nc.gpsimd.memset(deg[:, :], 1.0).then_inc(filled, 1)
            nc.gpsimd.memset(outside, 0.0).then_inc(filled, 1)
            nc.gpsimd.memset(bases[:, :], 0).then_inc(filled, 1)
            nc.gpsimd.memset(sel[:, :, :, SELS - 1, :], 0.0).then_inc(filled, 1)
            pool.wait_ge(consts, 3)
            nc.gpsimd.affine_select(out=ident[:, :], in_=ident[:, :], compare_op=ALU.not_equal, fill=1.0, base=0,
                                    pattern=[[-1, P]], channel_multiplier=1).then_inc(consts, 1)
            pool.wait_ge(consts, 4)
            for h in range(2):
                nc.gpsimd.tensor_copy(twice[:, h * LO:h * LO + LO], ident[0:LO, 0:LO]).then_inc(consts, 1)
            pool.wait_ge(el_split, 1)
            nc.gpsimd.tensor_tensor(el_flat, el_flat, el_bits[:, 0, :], ALU.subtract).then_inc(el_rest, 1)
            pool.wait_ge(w1_in, 16)
            nc.gpsimd.tensor_copy(w1_parts[:, 0, :], w1[:, :]).then_inc(w1_split, 1)
            pool.wait_ge(w1_split, 1)
            nc.gpsimd.tensor_tensor(w1_rest[:, :], w1[:, :], w1_parts[:, 0, :], ALU.subtract).then_inc(w1_rest_ready, 1)
            pool.wait_ge(w1_rest_ready, 1)
            nc.gpsimd.tensor_copy(w1_parts[:, 1, :], w1_rest[:, :]).then_inc(w1_split, 1)
            pool.wait_ge(w1_split, 2)
            nc.gpsimd.tensor_tensor(w1_parts[:, 2, :], w1_rest[:, :], w1_parts[:, 1, :], ALU.subtract).then_inc(w1_split, 1)
            pool.wait_ge(el_split, 2)
            pool.wait_ge(el_stored[0], 16)
            nc.gpsimd.tensor_tensor(el_bits[:, 0, :], el_flat, el_bits[:, 1, :], ALU.subtract).then_inc(el_split, 1)
            pool.wait_ge(hist_mm, 1)
            nc.gpsimd.memset(acc, 0.0).then_inc(acc_zeroed, 1)
            pool.wait_ge(src_in, 16)
            fl = flagged(pool)

            counts = [pool.alloc_register(f"count_{n}") for n in range(2)]

            def value(v, n):
                if isinstance(v, int):
                    return v
                pool.reg_mov(counts[n], v)
                return counts[n]

            def copy_idx(i, b):
                if not (isinstance(i, int) and i == 0):
                    pool.wait_ge(prod_done, i * 8 + (4 * b - 4))
                nc.gpsimd.tensor_copy(idx[:, b, :], src_i[:, bass.ds((i * 2 + b) * HALF, HALF)]).then_inc(idx_ready, 1)

            def body(i, first):
                for k in range(BODY):
                    b = k // HALF
                    if k % HALF == 0:
                        copy_idx(i, b)
                    copied = value(i * 2 + (b + 1), 0)
                    used = value(i * (BODY // 2) + ((k - SLOTS) // 2 + 1), 1)
                    pool.wait_ge(table_out, 5 * 16)
                    if k % HALF == 0:
                        pool.wait_ge(idx_ready, copied)
                    if not (first and k < SLOTS):
                        pool.wait_ge(prod_done, used)
                    nc.gpsimd.indirect_dma_start(
                        g_rows[:, k % SLOTS, :], None, table[:, :],
                        bass.IndirectOffsetOnAxis(idx[:, b, k % HALF:k % HALF + 1], 0)).then_inc(gathered[k % SLOTS], 16)

            with pool.If(fl == 0):
                body(0, True)
                with pool.Fori(1, ITERS) as i:
                    body(i, False)
            with pool.Else():
                def one_tile(t):
                    if not isinstance(t, int):
                        pool.wait_ge(g_prod, t)
                    nc.gpsimd.tensor_copy(idx[:, 0, 0:1], src_i[:, bass.ds(t, 1)]).then_inc(g_idx, 1)
                    copied = value(t + 1, 0)
                    pool.wait_ge(table_out, 5 * 16)
                    pool.wait_ge(g_idx, copied)
                    nc.gpsimd.indirect_dma_start(g_rows[:, 0, :], None, table[:, :],
                                                 bass.IndirectOffsetOnAxis(idx[:, 0, 0:1], 0)).then_inc(g_row, 16)

                one_tile(0)
                with pool.Fori(1, ET) as t:
                    one_tile(t)

        @block.tensor
        def _(pe):
            pe.wait_ge(consts, 6)
            pe.wait_ge(dstf_ready, 1)
            nc.tensor.matmul(base_ps, ones[0:1, :], dst_f[0:1, :], start=True, stop=True).then_inc(base_mm, 1)

            def transposes(t):
                pe.wait_ge(normed_ready, t + 1)
                if t >= 2:
                    pe.wait_ge(hT_ready, t - 1)
                for h in range(2):
                    last = nc.tensor.transpose(bank[6 + t % 2][:, h * P:h * P + P],
                                               normed[:, t % 4, h * P:h * P + P], ident[:, :])
                last.then_inc(trans_done, 1)

            def project(n):
                t = n % NT
                if n < NT:
                    pe.wait_ge(hT_ready, t + 1)
                if 4 <= n < NT + 4:
                    pe.wait_ge(f_scaled, n - 3)
                elif n >= NT + 4:
                    pe.wait_ge(res_done, n - NT - 3)
                for h in range(2):
                    last = nc.tensor.matmul(proj_ps(n)[:, h * P:h * P + P], hT[:, t, h * P:h * P + P],
                                            w_in[:, 2 * h + n // NT, :], start=True, stop=True)
                last.then_inc(proj_done, 1)

            def keep_warm(n):
                for _ in range(n):
                    nc.tensor.matmul(bank[5][:, 0:2 * P], ident[:, :], w_in[:, 0:2, :], start=True, stop=True)

            pe.wait_ge(blocks_in, 16)
            pe.wait_ge(onehots_near, 1)
            keep_warm(WARM)
            pe.wait_ge(onehots_ready, 1)
            for t in range(ET_FULL + 1):
                n = P if t < ET_FULL else LAST_EDGES
                last = nc.tensor.matmul(hist_ps, onehot[0:n, 0:LO, t], onehot[0:n, LO:LO + HI, t],
                                        start=(t == 0), stop=(t == ET_FULL))
            last.then_inc(hist_mm, 1)
            transposes(0)
            pe.wait_ge(hist_ready, 1)
            nc.tensor.matmul(deg_ps, twice[:, :], hist[:, :], start=True, stop=True).then_inc(deg_mm, 1)
            transposes(1)
            for t in range(2, NT + 2):
                project(t - 2)
                if t < NT:
                    transposes(t)
            pe.wait_ge(anyout_ready, 1)
            nc.tensor.matmul(out_ps, any_out[:, :], ones[:, 0:1], start=True, stop=True).then_inc(out_mm, 1)
            for t in range(NT):
                project(NT + t)

            fl = flagged(pe)
            pe.wait_ge(filled, 4)
            pe.wait_ge(w2_ready, 1)
            pe.wait_ge(w1_moved, 16 * PARTS * PARTS)

            def hidden(i, c):
                b = c // 2
                if c % 2 == 0:
                    pe.wait_ge(el_ready[b], i * (16 * PARTS) + 16 * PARTS)
                if not (isinstance(i, int) and 4 * i + c < 2):
                    pe.wait_ge(silu_done, i * 4 + (c - 1))
                nc.tensor.matmul(hid_ps[c % 2][0:HID, :], w1_stack[:, :], el[:, b, (c % 2) * 512:(c % 2) * 512 + 512],
                                 start=True, stop=True).then_inc(hid_mm, 1)

            def edge_weights(i, q):
                g = q // 2
                if q % 2 == 0:
                    pe.wait_ge(silu_done, i * 4 + (g + 1))
                if not (isinstance(i, int) and 8 * i + q < 4):
                    pe.wait_ge(prod_done, i * 8 + (q - 3))
                elif q == 0:
                    pe.wait_ge(res_done, NT)
                for tt in range(2):
                    e0 = (q % 2) * 2 * P + tt * P
                    last = nc.tensor.matmul(ew_ps[q % 4][:, tt, :], hid[:, g % 2, e0:e0 + P], w2[:, :],
                                            start=True, stop=True)
                last.then_inc(ew_mm, 1)

            def messages(i, q):
                pe.wait_ge(prod_done, i * 8 + (q + 1))
                if q % 4 == 0:
                    pe.wait_ge(sel_ready, i * 2 + (q // 4 + 1))
                if not (isinstance(i, int) and 8 * i + q < 2):
                    pe.wait_ge(add_done, i * 16 + 2 * (q - 1))
                for tt in range(2):
                    T = 2 * q + tt
                    pr = prods[:, q % XB, tt, :, :].rearrange("p b u -> p (b u)")
                    s = sel[:, (T // HALF) % 2, T % HALF, :, :]
                    for block, g in MESSAGES:
                        last = nc.tensor.matmul(msg_ps[q % 2][:, tt, g:g + SELS, :], pr[:, block * MUL:block * MUL + P], s,
                                                start=True, stop=True)
                last.then_inc(msg_mm, 1)

            def body(i):
                for c in range(4):
                    hidden(i, c)
                    for q in (2 * c - 2, 2 * c - 1):
                        if not (isinstance(i, int) and q < 0):
                            edge_weights(*at_pair(i, q))
                        if not (isinstance(i, int) and q < LAG):
                            messages(*at_pair(i, q - LAG))

            with pe.If(fl == 0):
                body(0)
                with pe.Fori(1, ITERS) as i:
                    body(i)
                for q in (6, 7, 8, 9):
                    if q < 8:
                        edge_weights(ITERS - 1, q)
                    messages(ITERS - 1, q - LAG)
            with pe.Else():
                with pe.Fori(0, ET) as t:
                    pe.wait_ge(g_el, t * (16 * PARTS) + 16 * PARTS)
                    nc.tensor.matmul(hid_ps[0][0:HID, 0:P], w1_stack[:, :], el[:, 0, 0:P],
                                     start=True, stop=True).then_inc(g_hid, 1)
                    pe.wait_ge(g_silu, t + 1)
                    pe.wait_ge(res_done, NT)
                    nc.tensor.matmul(ew_ps[0][:, 0, :], hid[:, 0, 0:P], w2[:, :], start=True, stop=True).then_inc(g_ew, 1)
                    pe.wait_ge(acc_zeroed, 1)
                    pe.wait_ge(g_prod, t + 1)
                    with pe.Fori(0, NT) as w:
                        pe.wait_ge(g_sel, t * NT + w + 1)
                        pr = prods[:, 0, 0, :, :].rearrange("p b u -> p (b u)")
                        for block, k, g in GENERAL:
                            into = bank[6 + g // 4][:, g % 4 * P:g % 4 * P + P]
                            last = nc.tensor.matmul(into, pr[:, block * MUL:block * MUL + P],
                                                    slow_sel[:, k, :], start=True, stop=True)
                        last.then_inc(g_msg, 1)

            keep_warm(WARM_END)
            pe.wait_ge(acc_ready, 1)
            for t in range(NT + LEAD):
                if t < NT:
                    if t >= 8:
                        pe.wait_ge(fin_done, t - 7)
                    for g, group in enumerate((4, 5)):
                        last = nc.tensor.matmul(bank[t % 8][:, g * P:g * P + P], acc[:, group, t * P:t * P + P],
                                                lo_w[:, g, :], start=(g == 0), stop=False)
                n = t - LEAD
                if n >= 0:
                    if n in M_CHUNKS:
                        pe.wait_ge(moved[M_CHUNKS.index(n)], 32)
                    for g, group in enumerate((0, 2)):
                        last = nc.tensor.matmul(bank[n % 8][:, g * P:g * P + P], acc[:, group, n * P:n * P + P],
                                                lo_w[:, 2 + g, :], start=False, stop=(g == 1))
                    last.then_inc(fin_mm, 1)

        @block.scalar
        def _(act):
            act.dma_start(attr[:, :], attr_t).then_inc(attr_in, 16)
            act.dma_start(w1[:, :], w_mlp1).then_inc(w1_in, 16)
            act.dma_start(blocks[:, :, :], w_blocks.rearrange("p (n f) -> p n f", n=8)).then_inc(blocks_in, 16)
            act.dma_start(w2_raw[:, :], w_mlp2).then_inc(w2_in, 16)

            def transposed(t):
                act.wait_ge(trans_done, t + 1)
                nc.scalar.activation(hT[:, t, :], bank[6 + t % 2][:, 0:WIDTH], ACT.Relu).then_inc(hT_ready, 1)

            act.wait_ge(el_in, 16)
            nc.scalar.activation(el_bits[:, 0, :], el_flat, ACT.Copy).then_inc(el_split, 1)
            act.wait_ge(el_rest, 1)
            nc.scalar.activation(el_bits[:, 1, :], el_flat, ACT.Copy).then_inc(el_split, 1)
            act.wait_ge(stats_ready, 1)
            nc.scalar.activation(std[:, :], mean_var[:, :, 1], ACT.Sqrt).then_inc(std_ready, 1)
            act.wait_ge(el_split, 3)
            act.wait_ge(onehots_ready, 1)
            transposed(0)
            act.wait_ge(deg_ready, 1)
            nc.scalar.activation(sdeg[:, :], deg[:, :], ACT.Sqrt).then_inc(sdeg_ready, 1)
            transposed(1)
            act.wait_ge(cf_ready, 1)
            act.wait_ge(hist_mm, 1)
            transposed(2)
            for t in range(NT):
                act.wait_ge(proj_done, t + 1)
                if t == NT - LATE:
                    act.wait_ge(anyout_ready, 1)
                nc.scalar.activation(f_rows[:, t, :], proj_ps(t), ACT.Copy, scale=c_f[:, t:t + 1]).then_inc(f_scaled, 1)
                if t < NT - 3:
                    transposed(t + 3)

            nc.scalar.activation(warm[:, :], sdeg[0:1, 0:1], ACT.Silu)

            fl = flagged(act)

            def silu(i, c):
                act.wait_ge(hid_mm, i * 4 + (c + 1))
                if not (isinstance(i, int) and 4 * i + c < 2):
                    act.wait_ge(ew_mm, i * 8 + (2 * c - 2))
                nc.scalar.activation(hid[:, c % 2, :], hid_ps[c % 2][0:HID, :], ACT.Silu,
                                     scale=1.0 / math.sqrt(BASIS)).then_inc(silu_done, 1)

            def scale_rows(out, slot, y):
                for m in range(3):
                    last = nc.scalar.activation(out[:, m, :], g_rows[:, slot, (1 + m) * MUL:(2 + m) * MUL], ACT.Copy,
                                                scale=y(1 + m))
                return last

            def scaled_rows(i, q):
                if not (isinstance(i, int) and 8 * i + q < XB):
                    act.wait_ge(prod_done, i * 8 + (q + 1 - XB))
                for tt in range(2):
                    T = 2 * q + tt
                    act.wait_ge(gathered[T % SLOTS], i * (16 * BODY // SLOTS) + 16 * (T // SLOTS + 1))
                    last = scale_rows(gy[:, q % XB, tt], T % SLOTS, lambda k: y_at(i, T, k))
                last.then_inc(gy_ready, 1)

            def y_at(i, T, k):
                if isinstance(i, int):
                    return y_sb[:, i * BODY + T, k:k + 1]
                return y_flat[:, bass.ds((i * BODY + T) * 4 + k, 1)]

            def body(i):
                for c in range(4):
                    first = isinstance(i, int) and c == 0
                    if not first:
                        silu(i, c)
                    for q in (2 * c, 2 * c + 1):
                        scaled_rows(i, q)
                    if first:
                        silu(i, c)

            act.wait_ge(y_in, 16)
            with act.If(fl == 0):
                body(0)
                with act.Fori(1, ITERS) as i:
                    body(i)
            with act.Else():
                def one_tile(t):
                    act.wait_ge(g_hid, t + 1)
                    if not isinstance(t, int):
                        act.wait_ge(g_ew, t)
                        act.wait_ge(g_prod, t)
                    nc.scalar.activation(hid[:, 0, 0:P], hid_ps[0][0:HID, 0:P], ACT.Silu,
                                         scale=1.0 / math.sqrt(BASIS)).then_inc(g_silu, 1)
                    act.wait_ge(g_row, t * 16 + 16)
                    scale_rows(gy[:, 0, 0], 0, lambda k: y_flat[:, bass.ds(t * 4 + k, 1)]).then_inc(g_gy, 1)

                one_tile(0)
                with act.Fori(1, ET) as t:
                    one_tile(t)

            act.wait_ge(acc_ready, 1)
            for c in range(5):
                nodes = slice(M_CHUNKS[c] * P, M_CHUNKS[c + 1] * P)
                act.dma_start(acc[0:MUL, 0, nodes], acc[0:MUL, 1, nodes]).then_inc(moved[c], 16)

        @block.vector
        def _(dve):
            chain = [0]

            def link(ins):
                chain[0] += 1
                ins.then_inc(v_step, 1)
                dve.wait_ge(v_step, chain[0])

            dve.wait_ge(dst_in, 16)
            nc.vector.tensor_copy(dst_f[:, :], dst_i[:, :]).then_inc(dstf_ready, 1)
            nc.vector.tensor_scalar(parts_i[:, 0, :], dst_i[:, :], LO - 1, None, ALU.bitwise_and)
            link(nc.vector.tensor_scalar(parts_i[:, 1, :], dst_i[:, :], LO_BITS, None, ALU.arith_shift_right))
            link(nc.vector.tensor_copy(parts_b, parts_i))
            for j in range(HI):
                last = nc.vector.tensor_scalar(onehot[:, j:j + LO + 1:LO, :], parts_b, float(j), None, ALU.is_equal)
                if j == HI - NEAR:
                    last.then_inc(onehots_near, 1)
            for j in range(HI, LO):
                last = nc.vector.tensor_scalar(onehot[:, j, :], parts_b[:, 0, :], float(j), None, ALU.is_equal)
            last.then_inc(onehots_ready, 1)

            for t in range(NT):
                if t in X_CHUNKS:
                    dve.wait_ge(x_in[X_CHUNKS.index(t)], 16)
                last = nc.vector.bn_stats(stats[:, t, :], x_sb[:, t, :])
            link(last)
            for t in range(NT):
                last = nc.vector.bn_aggr(mean_var[:, t, :], stats[:, t, :])
            link(last)
            nc.vector.tensor_scalar(mean_var[:, :, 1], mean_var[:, :, 1], EPS, None, ALU.add).then_inc(stats_ready, 1)
            dve.wait_ge(attr_in, 16)
            link(nc.vector.tensor_scalar(a8[:, :], attr[:, :], 1.0 / math.sqrt(MUL), None, ALU.mult))
            nc.vector.tensor_scalar(c_m[:, :], a8[:, :], C_S, None, ALU.mult)
            dve.wait_ge(std_ready, 1)
            link(nc.vector.reciprocal(rstd[:, :], std[:, :]))
            link(nc.vector.scalar_tensor_tensor(shift[:, :], mean_var[:, :, 0], -1.0, rstd[:, :], ALU.mult, ALU.mult))

            def normalise(t):
                if t >= 4:
                    dve.wait_ge(trans_done, t - 3)
                nc.vector.tensor_scalar(normed[:, t % 4, :], x_sb[:, t, :], rstd[:, t:t + 1], shift[:, t:t + 1],
                                        ALU.mult, ALU.add).then_inc(normed_ready, 1)

            normalise(0)
            dve.wait_ge(hist_mm, 1)
            dve.wait_ge(filled, 3)
            nc.vector.tensor_copy(hist[:, :], hist_ps).then_inc(hist_ready, 1)
            normalise(1)
            dve.wait_ge(deg_mm, 1)
            pairs = deg_ps.rearrange("p (t r) -> p t r", r=2)
            nc.vector.tensor_scalar(deg[0:MUL, 0:NT], pairs[0:MUL, 0:NT, 0], 1.0, None, ALU.max)
            nc.vector.tensor_scalar(deg[MUL:P, 0:NT], pairs[MUL:P, 0:NT, 1], 1.0, None, ALU.max).then_inc(deg_ready, 1)
            normalise(2)
            dve.wait_ge(sdeg_ready, 1)
            link(nc.vector.reciprocal(isq[:, :], sdeg[:, :]))
            nc.vector.tensor_tensor(c_f[:, :], a8[:, :], isq[:, :], ALU.mult).then_inc(cf_ready, 1)
            dve.wait_ge(cf_ready, 1)
            link(nc.vector.tensor_scalar(c_o[:, :], c_f[:, :], C_X * math.sqrt(MUL) / math.sqrt(2 * MUL), None, ALU.mult))

            for t in range(3, NT):
                normalise(t)
                if t == 4:
                    dve.wait_ge(base_mm, 1)
                    link(nc.vector.tensor_tensor(rel[:, :], dst_f[:, :], base_ps, ALU.subtract))
                elif t == 6:
                    link(nc.vector.tensor_scalar(below, rel[:, :], 0.0, None, ALU.is_lt))
                elif t == 8:
                    for n, cols in ((P, slice(0, ET_FULL)), (LAST_EDGES, slice(ET_FULL, ET_FULL + 1))):
                        last = nc.vector.scalar_tensor_tensor(outside[0:n, cols], rel[0:n, cols], WIN - 0.5, below[0:n, cols],
                                                              ALU.is_gt, ALU.add)
                elif t == 10:
                    link(last)
                    nc.vector.reduce_max(any_out[:, :], outside, AX.X).then_inc(anyout_ready, 1)
                elif t == 12:
                    nc.vector.tensor_copy(bases[0:1, 2 * LAG:2 * LAG + ET], dst_i[0:1, :]).then_inc(bases_ready, 1)
                elif t == 14:
                    dve.wait_ge(w2_in, 16)
                    k = 1.0 / math.sqrt(HID)
                    for n, (o, s) in enumerate(((0, k), (2, k), (3, k), (1, k / math.sqrt(3.0)))):
                        last = nc.vector.tensor_scalar(w2[:, n * MUL:(n + 1) * MUL], w2_raw[:, o * MUL:(o + 1) * MUL], s, None, ALU.mult)
                    last.then_inc(w2_ready, 1)
            def select(i, b):
                T0 = (i * 2 + b) * HALF
                if not (isinstance(i, int) and i == 0):
                    dve.wait_ge(msg_mm, i * 8 + 4 * (b - 1))
                n = [P, HALF, WIN]
                one = sel[:, b, :, 1, :]
                nc.vector.tensor_tensor(one, iota[:, 0:WIN].unsqueeze(1).broadcast_to(n),
                                        rel[:, bass.ds(T0, HALF)].unsqueeze(2).broadcast_to(n),
                                        ALU.is_equal).then_inc(oh_done, 1)
                dve.wait_ge(oh_done, i * 2 + (b + 1))
                y = y_sb[:, bass.ds(T0, HALF), :]
                nc.vector.tensor_tensor(sel[:, b, :, 0, :], one, y[:, :, 0].unsqueeze(2).broadcast_to(n), ALU.mult)
                n = [P, HALF, 3, WIN]
                nc.vector.tensor_tensor(sel[:, b, :, 2:5, :], one.unsqueeze(2).broadcast_to(n),
                                        y[:, :, 1:4].unsqueeze(3).broadcast_to(n), ALU.mult).then_inc(sel_ready, 1)

            dve.wait_ge(y_in, 16)
            dve.wait_ge(consts, 2)
            select(0, 0)
            select(0, 1)

            dve.wait_ge(out_mm, 1)
            nc.vector.tensor_scalar(flag[:, :], out_ps, 1.0, None, ALU.min).then_inc(flag_ready, 1)

            for t in range(NT):
                dve.wait_ge(proj_done, NT + t + 1)
                nc.vector.scalar_tensor_tensor(x_sb[:, t, :], proj_ps(NT + t), c_m[:, t:t + 1], x_sb[:, t, :],
                                               ALU.mult, ALU.add).then_inc(res_done, 1)

            fl = flagged(dve)
            dve.wait_ge(acc_zeroed, 1)
            dve.wait_ge(bases_ready, 1)

            def products(i, q, meanwhile):
                dve.wait_ge(ew_mm, i * 8 + (q + 1))
                for s in ((2 * q) % SLOTS, (2 * q + 1) % SLOTS):
                    dve.wait_ge(gathered[s], i * (16 * BODY // SLOTS) + 16 * (2 * q // SLOTS + 1))
                if not (isinstance(i, int) and 8 * i + q < XB):
                    dve.wait_ge(msg_mm, i * 8 + (q + 1 - XB))
                dve.wait_ge(gy_ready, i * 8 + (q + 1))
                multiply(prods[:, q % XB], ew_ps[q % 4], gy[:, q % XB], (2 * q) % SLOTS, 2, q_step, i * 16 + 2 * q,
                         meanwhile).then_inc(prod_done, 1)

            def multiply(pr, ew, gy_, s0, tiles, step, steps, meanwhile=lambda n: None):
                dot = gy_[:, 0:tiles, 0, :]
                nc.vector.tensor_tensor(dot, dot, gy_[:, 0:tiles, 1, :], ALU.add).then_inc(step, 1)
                g0 = g_rows[:, s0:s0 + tiles, 0:MUL]
                n = [P, tiles, 2, MUL]
                nc.vector.tensor_tensor(pr[:, 0:tiles, 0:5:4, :], ew[:, 0:tiles, 0:2 * MUL].rearrange("p t (b u) -> p t b u", b=2),
                                        g0.unsqueeze(2).broadcast_to(n), ALU.mult)
                meanwhile(0)
                dve.wait_ge(step, steps + 1)
                nc.vector.tensor_tensor(dot, dot, gy_[:, 0:tiles, 2, :], ALU.add).then_inc(step, 1)
                g1 = g_rows[:, s0:s0 + tiles, MUL:].rearrange("p t (m u) -> p t m u", m=3)
                n = [P, tiles, 3, MUL]
                nc.vector.tensor_tensor(pr[:, 0:tiles, 1:4, :], ew[:, 0:tiles, 2 * MUL:3 * MUL].unsqueeze(2).broadcast_to(n),
                                        g1, ALU.mult)
                meanwhile(1)
                dve.wait_ge(step, steps + 2)
                return nc.vector.tensor_tensor(pr[:, 0:tiles, 5, :], ew[:, 0:tiles, 3 * MUL:], dot, ALU.mult)

            def add(i, q, tt, base):
                if tt == 0:
                    dve.wait_ge(msg_mm, i * 8 + (q + 1))
                T = 2 * q + tt
                if not (isinstance(i, int) and 16 * i + T < 1):
                    dve.wait_ge(add_done, i * 16 + T)
                win = acc[:, :, bass.ds(base, WIN)]
                nc.vector.tensor_tensor(win, win, msg_ps[q % 2][:, tt, 1:1 + GROUPS, :], ALU.add).then_inc(add_done, 1)

            base_regs = [dve.alloc_register(f"base_{k}") for k in range(BODY)]

            def load_bases(at, n, r=0):
                regs = base_regs[r:r + n]
                dve.load(regs, bases[0:1, at if isinstance(at, slice) else bass.ds(at, n)])
                return [dve.snap(r, min_val=0, max_val=NODES - 1) for r in regs]

            def body(i):
                base = []
                for q in range(8):
                    if q % 4 == 0 and not isinstance(i, int):
                        select(i, q // 4)
                    if q % 2 == 0:
                        base += load_bases(i * BODY + 2 * q, 4, 2 * q)
                    late = not (isinstance(i, int) and q < LAG)
                    products(i, q, lambda tt: late and add(*at_pair(i, q - LAG), tt, base[2 * q + tt]))

            with dve.If(fl == 0):
                body(0)
                with dve.Fori(1, ITERS) as i:
                    body(i)
                base = load_bases(ITERS * BODY, 2 * LAG)
                for q in range(LAG):
                    for tt in range(2):
                        add(ITERS - 1, 8 - LAG + q, tt, base[2 * q + tt])
                dve.wait_ge(add_done, ET)
                nc.vector.memset(any_out[:, :], 0.0).then_inc(acc_ready, 1)
            with dve.Else():
                with dve.Fori(0, ET) as t:
                    dve.wait_ge(g_ew, t + 1)
                    dve.wait_ge(g_row, t * 16 + 16)
                    dve.wait_ge(g_gy, t + 1)
                    multiply(prods[:, 0], ew_ps[0], gy[:, 0], 0, 1, g_q, t * 2).then_inc(g_prod, 1)
                    nc.vector.tensor_copy(slow_dst[:, :], dst_f[:, bass.ds(t, 1)]).then_inc(g_chain, 1)
                    with dve.Fori(0, NT) as w:
                        done = t * NT + w
                        dve.wait_ge(g_chain, done + t + 1)
                        nc.vector.tensor_scalar(slow_sel[:, 1, :], iota[:, :], slow_dst[:, 0:1], None, ALU.is_equal)
                        for k in range(4):
                            last = nc.vector.tensor_scalar(slow_sel[:, k + min(k, 1), :], iota[:, :], slow_dst[:, 0:1],
                                                           y_sb[:, bass.ds(t, 1), k], ALU.is_equal, ALU.mult)
                        last.then_inc(g_sel, 1)
                        dve.wait_ge(g_sel, done + 1)
                        nc.vector.tensor_scalar(slow_dst[:, :], slow_dst[:, :], float(-P), None, ALU.add).then_inc(g_chain, 1)
                        dve.wait_ge(g_msg, done + 1)
                        win = acc[:, 0:4, bass.ds(w * P, P)]
                        nc.vector.tensor_tensor(win, win, bank[6][:, :].rearrange("p (g n) -> p g n", g=4), ALU.add)
                        win = acc[:, 4:6, bass.ds(w * P, P)]
                        nc.vector.tensor_tensor(win, win, bank[7][:, 0:2 * P].rearrange("p (g n) -> p g n", g=2), ALU.add).then_inc(g_add, 1)
                        dve.wait_ge(g_add, done + 1)
                nc.vector.memset(any_out[:, :], 0.0).then_inc(acc_ready, 1)

            for t in range(NT):
                dve.wait_ge(fin_mm, t + 1)
                if t >= O_RING:
                    dve.wait_ge(o_out[t % O_RING], 16 * (t // O_RING))
                nc.vector.scalar_tensor_tensor(o_sb[:, t % O_RING, :], bank[t % 8][:, 0:WIDTH], c_o[:, t:t + 1], x_sb[:, t, :],
                                               ALU.mult, ALU.add).then_inc(fin_done, 1)


MESSAGES = ((4, 0), (0, 5), (2, 6))
GENERAL = ((4, 1, 0), (4, 2, 1), (4, 3, 2), (4, 4, 3), (0, 0, 4), (2, 0, 5))


def at_pair(i, q):
    return (i - 1, q + 8) if q < 0 else (i, q)


def kernel(x, src, dst, edge_attr_10, edge_attr_4, node_vec1, L0_gnn_W_li0, L0_gnn_W_li1, L0_gnn_W_lm0, L0_gnn_W_lm1,
           L0_gnn_W_mlp1, L0_gnn_W_mlp2, L0_gnn_W_lo0, L0_gnn_W_lo1):
    import numpy as np
    import concourse.bacc as bacc
    from concourse.bass_utils import run_bass_kernel_spmd

    def padded(a, rows):
        out = np.zeros((rows,) + a.shape[1:], a.dtype)
        out[:a.shape[0]] = a
        return out

    x, src, dst = np.asarray(x), np.asarray(src), np.asarray(dst)
    nodes = np.concatenate([x[:, :MUL], x[:, MUL:].reshape(NODES, MUL, 3).transpose(0, 2, 1).reshape(NODES, 3 * MUL)], axis=1)
    li0, li1, lm0, lm1, lo0, lo1 = (np.asarray(w) for w in (L0_gnn_W_li0, L0_gnn_W_li1, L0_gnn_W_lm0, L0_gnn_W_lm1,
                                                            L0_gnn_W_lo0, L0_gnn_W_lo1))
    blocks = np.zeros((P, 8, P), li0.dtype)
    for n, upper, lower in ((0, li0, li1), (1, lm0, lm1), (2, li1, li1), (3, lm1, lm1), (4, lo0[:MUL], lo1[MUL:]),
                            (5, lo1[MUL:], lo1[MUL:]), (7, lo1[:MUL], lo1[:MUL])):
        blocks[:MUL, n, :MUL] = upper
        blocks[MUL:, n, MUL:] = lower
    blocks[:MUL, 6, MUL:] = lo1[:MUL]
    blocks[MUL:, 6, :MUL] = lo0[MUL:]
    arrays = {
        "in_x": padded(nodes, NODES_PAD),
        "in_src": np.ascontiguousarray(padded(src, EDGES_PAD).reshape(ET, P).T),
        "in_dst": np.ascontiguousarray(padded(dst, EDGES_PAD).reshape(ET, P).T),
        "in_el": np.ascontiguousarray(padded(np.asarray(edge_attr_10), EDGES_PAD).T),
        "in_y": np.ascontiguousarray(padded(np.asarray(edge_attr_4), EDGES_PAD).reshape(ET, P, 4).transpose(1, 0, 2).reshape(P, ET * 4)),
        "in_attr": np.ascontiguousarray(padded(np.asarray(node_vec1), NODES_PAD).reshape(NT, P).T),
        "in_blocks": blocks.reshape(P, 8 * P),
        "in_mlp1": np.asarray(L0_gnn_W_mlp1), "in_mlp2": np.asarray(L0_gnn_W_mlp2),
    }
    nc = bacc.Bacc("TRN2", target_bir_lowering=False, num_devices=1)
    args = [nc.dram_tensor(n, a.shape, mybir.dt.from_np(a.dtype), kind="ExternalInput").ap() for n, a in arrays.items()]
    out = nc.dram_tensor("out_nodes", (NODES_PAD, WIDTH), mybir.dt.float32, kind="ExternalOutput").ap()
    gnn_layer(nc, *args, out)
    r = run_bass_kernel_spmd(nc, [arrays], core_ids=[0])
    got = np.asarray(r.results[0]["out_nodes"])[:NODES]
    vec = got[:, MUL:].reshape(NODES, 3, MUL).transpose(0, 2, 1).reshape(NODES, 3 * MUL)
    return np.concatenate([got[:, :MUL], vec], axis=1)
```
